# Optimizing a Trainium2 kernel written in Bass

```python
import numpy as np
import jax
import jax.numpy as jnp

def _softmax(x, axis=-1):
    return jax.nn.softmax(x, axis=axis)

def _gelu(x):
    return jax.nn.gelu(x, approximate=True)

def _silu(x):
    return jax.nn.silu(x)

def _sigmoid(x):
    return jax.nn.sigmoid(x)

def _layernorm(x, axis=-1, eps=1e-05):
    m = jnp.mean(x, axis=axis, keepdims=True)
    v = jnp.var(x, axis=axis, keepdims=True)
    return (x - m) / jnp.sqrt(v + eps)

def _scatter_add(tgt, idx, src, axis=0):
    return tgt.at[idx].add(src)

def _segment_sum(src, seg, n):
    return jax.ops.segment_sum(src, seg, n)
kernel_name = 'mk_gnn_preln_d2_gnn_r32_273e48'

def setup_inputs(seed: int=0):
    np.random.seed(seed)
    _w = jnp.asarray

    def _rec_inputs():
        import jax
        import jax.numpy as jnp
        _gk = jax.random.key(seed)
        x = -0.000202 + 1 * jax.random.normal(jax.random.fold_in(_gk, 1), (50000, 128), jnp.float32)
        src = jax.random.randint(jax.random.fold_in(_gk, 2), (25000,), 0, 50000, jnp.int32)
        dst = jax.random.randint(jax.random.fold_in(_gk, 3), (25000,), 0, 50000, jnp.int32)
        _o = jnp.argsort(dst, stable=True)
        src = src[_o]
        dst = dst[_o]
        edge_attr_128 = -8.513e-05 + 0.999844 * jax.random.normal(jax.random.fold_in(_gk, 12), (25000, 128), jnp.float32)
        return (x, src, dst, edge_attr_128)
    x, src, dst, edge_attr_128 = _rec_inputs()

    def _L0_gnn_setup():
        import jax, jax.numpy as jnp
        import numpy as np
        N_NODES = 50000
        N_EDGES = 20000
        D_IN = 128
        D_OUT = 128
        key = jax.random.key(seed)
        ks = jax.random.split(key, 8)
        scale_in = 1.0 / np.sqrt(D_IN)
        return {'x': jax.random.normal(ks[0], (N_NODES, D_IN), dtype=jnp.float32), 'r_feat': jax.random.normal(ks[1], (N_EDGES, D_IN), dtype=jnp.float32), 'src': jax.random.randint(ks[2], (N_EDGES,), 0, N_NODES), 'dst': jax.random.randint(ks[3], (N_EDGES,), 0, N_NODES), 'w': jax.random.normal(ks[4], (D_OUT, D_IN), dtype=jnp.float32) * scale_in, 'w_r': jax.random.normal(ks[5], (D_OUT, D_IN), dtype=jnp.float32) * scale_in, 'att_w': jax.random.normal(ks[6], (3 * D_OUT,), dtype=jnp.float32) * (1.0 / np.sqrt(3 * D_OUT)), 'loop_w': jax.random.normal(ks[7], (D_OUT, D_OUT), dtype=jnp.float32) * (1.0 / np.sqrt(D_OUT))}
    _L0_gnn_all = _L0_gnn_setup()
    _L0_gnn_in = {k: v for k, v in _L0_gnn_all.items() if k in ('w', 'w_r', 'att_w', 'loop_w')}
    del _L0_gnn_all

    def _L1_gnn_setup():
        import jax, jax.numpy as jnp
        import numpy as np
        LOG2 = float(np.log(2.0))

        def ssp(x):
            return jax.nn.softplus(x) - LOG2
        key = jax.random.key(seed)
        ks = jax.random.split(key, 8)
        N, E, H, F = (50000, 50000, 128, 128)
        h = jax.random.normal(ks[0], (N, H), dtype=jnp.float32)
        edge_index = jax.random.randint(ks[1], (2, E), 0, N, dtype=jnp.int64)
        edge_attr = jax.random.normal(ks[2], (E, H), dtype=jnp.float32)

        def xavier(k, shape):
            fan_in, fan_out = (shape[1], shape[0])
            bound = float(np.sqrt(6.0 / (fan_in + fan_out)))
            return jax.random.uniform(k, shape, jnp.float32, -bound, bound)
        fc1_w = xavier(ks[3], (F, H))
        w1 = xavier(ks[4], (F, H))
        b1 = jnp.zeros((F,), jnp.float32)
        w2 = xavier(ks[5], (F, F))
        b2 = jnp.zeros((F,), jnp.float32)
        return {'h': h, 'edge_index': edge_index, 'edge_attr': edge_attr, 'fc1_w': fc1_w, 'w1': w1, 'b1': b1, 'w2': w2, 'b2': b2}
    _L1_gnn_all = _L1_gnn_setup()
    _L1_gnn_in = {k: v for k, v in _L1_gnn_all.items() if k in ('fc1_w', 'w1', 'b1', 'w2', 'b2')}
    del _L1_gnn_all
    return {'x': x, 'src': src, 'dst': dst, 'edge_attr_128': edge_attr_128, 'L0_gnn_w': _L0_gnn_in['w'], 'L0_gnn_w_r': _L0_gnn_in['w_r'], 'L0_gnn_att_w': _L0_gnn_in['att_w'], 'L0_gnn_loop_w': _L0_gnn_in['loop_w'], 'L1_gnn_fc1_w': _L1_gnn_in['fc1_w'], 'L1_gnn_w1': _L1_gnn_in['w1'], 'L1_gnn_b1': _L1_gnn_in['b1'], 'L1_gnn_w2': _L1_gnn_in['w2'], 'L1_gnn_b2': _L1_gnn_in['b2']}

def reference(x, src, dst, edge_attr_128, L0_gnn_w, L0_gnn_w_r, L0_gnn_att_w, L0_gnn_loop_w, L1_gnn_fc1_w, L1_gnn_w1, L1_gnn_b1, L1_gnn_w2, L1_gnn_b2):
    import jax
    import jax.numpy as jnp

    def _L0_gnn_ref(x, r_feat, src, dst, w, w_r, att_w, loop_w):
        import jax, jax.numpy as jnp
        import numpy as np
        N_NODES = 50000
        N_EDGES = 20000
        D_IN = 128
        D_OUT = 128
        n = x.shape[0]
        h = x @ w.T
        rh = r_feat @ w_r.T
        d = h.shape[1]
        s_src = h @ att_w[:d]
        s_dst = h @ att_w[d:2 * d]
        s_rel = rh @ att_w[2 * d:]
        e = jax.nn.leaky_relu(s_src[src] + s_dst[dst] + s_rel)
        m = jax.ops.segment_max(e, dst, num_segments=n)
        ex = jnp.exp(e - m[dst])
        denom = jax.ops.segment_sum(ex, dst, num_segments=n)
        alpha = ex / denom[dst]
        msg = alpha[:, None] * (h[src] + rh)
        agg = jax.ops.segment_sum(msg, dst, num_segments=n)
        deg = jax.ops.segment_sum(jnp.ones_like(e), dst, num_segments=n)
        h_out = jnp.where(deg[:, None] > 0, agg + h @ loop_w, h)
        return jax.nn.relu(h_out)

    def _L1_gnn_ref(h, edge_index, edge_attr, fc1_w, w1, b1, w2, b2):
        import jax, jax.numpy as jnp
        import numpy as np
        LOG2 = float(np.log(2.0))

        def ssp(x):
            return jax.nn.softplus(x) - LOG2
        N = h.shape[0]
        W = ssp(edge_attr @ w1.T + b1)
        W = ssp(W @ w2.T + b2)
        src, dst = (edge_index[0], edge_index[1])
        x_j = h[src]
        msg = x_j @ fc1_w.T * W
        out = jax.ops.segment_sum(msg, dst, num_segments=N)
        return out
    edge_index = jnp.stack([src, dst])
    h = jnp.maximum(_layernorm(x, axis=-1), 0.0)
    x = x + _L0_gnn_ref(h, edge_attr_128, src, dst, L0_gnn_w, L0_gnn_w_r, L0_gnn_att_w, L0_gnn_loop_w)
    h = jnp.maximum(_layernorm(x, axis=-1), 0.0)
    x = x + _L1_gnn_ref(h, edge_index, edge_attr_128, L1_gnn_fc1_w, L1_gnn_w1, L1_gnn_b1, L1_gnn_w2, L1_gnn_b2)
    return x

_drawn_inputs = setup_inputs


def setup_inputs(seed=0):
    import zlib

    import numpy as np

    out = dict(_drawn_inputs(seed))
    spreads = {'L1_gnn_b1': (0.0, 0.72), 'L1_gnn_b2': (0.0, 0.316)}
    factors = {}
    for name, (base, spread) in spreads.items():
        noise = np.random.default_rng([zlib.crc32(name.encode()), seed]).standard_normal(out[name].shape)
        drawn = base * np.exp(spread * noise) if base else spread * noise
        out[name] = jnp.asarray(drawn.astype(out[name].dtype))
    for name, factor in factors.items():
        out[name] = (out[name] * factor).astype(out[name].dtype)
    return out
```

```python
from contextlib import ExitStack

import concourse.bass as bass
from concourse import mybir

ALU = mybir.AluOpType
ACT = mybir.ActivationFunctionType
AX = mybir.AxisListType
F32 = mybir.dt.float32
I32 = mybir.dt.int32

P = 128
D = 128
DX = D + 1
ET = 4
NT = 8
LT = 2 * ET + NT
EPS = 1e-5
LOG2 = 0.6931471805599453
CAP = 40.0
FAR = 1e30
PAD_DST = 60000.0
NORM_ACT = 8
NORM_DVE = LT - NORM_ACT
SM_BCAST = 9
SM_SHIFTED = 8 + 4 + 2 + 16 + 3 + 2 + 2
SKIP = 100000.0


def wait(eng, sem, value):
    if not (isinstance(value, int) and value <= 0):
        eng.wait_ge(sem, value)


def wait_apart(eng, sem, value):
    wait(eng, sem, value)
    if not isinstance(value, int):
        eng.nop(nofuse=True)


def pipelined(eng, groups, first, second):
    assert groups % 2 == 1
    first((0, 0, 0))
    first((1, 1, 0))
    second((0, 0, 0))
    with eng.Fori(0, (groups - 3) // 2) as k:
        first((2 * k + 2, 0, k + 1))
        second((2 * k + 1, 1, k))
        first((2 * k + 3, 1, k + 1))
        second((2 * k + 2, 0, k + 1))
    last = groups - 1
    first((last, 0, last // 2))
    second((last - 1, 1, last // 2 - 1))
    second((last, 0, last // 2))


def in_turn(eng, groups, step):
    step((0, 0, 0))
    step((1, 1, 0))
    with eng.Fori(1, (groups - 1) // 2) as k:
        step((2 * k, 0, k))
        step((2 * k + 1, 1, k))
    step((groups - 1, 0, (groups - 1) // 2))


def gnn_kernel(nc, x, src, dst, ea, w, w_r, att_w, loop_w, fc1_w, w1, b1, w2, b2, out):
    N = x.shape[0]
    E = src.shape[0]
    TILES = -(-E // P)
    HALF = TILES // 2
    GROUPS = TILES // ET
    EG = ET * P
    NG = NT * P
    REST = E - (TILES - 1) * P
    assert TILES == 2 * HALF == ET * GROUPS and GROUPS % 2 == 1 and HALF <= P and 0 < REST < P
    assert (GROUPS - 1) * NG < N <= GROUPS * NG
    LAST_NODE = N - NG
    SLOT_USES = [GROUPS // 2 + 1, GROUPS // 2]

    ctx = ExitStack()
    with ctx:
        def sb(name, shape, dt=F32):
            return ctx.enter_context(nc.sbuf_tensor(name, shape, dt))

        def sem(name):
            return ctx.enter_context(nc.semaphore(name))

        def sem2(name):
            return [sem(f"{name}{b}") for b in range(2)]

        mg_dram = nc.dram_tensor("mg_scratch", [GROUPS, P, 2 * ET * DX], F32, kind="Internal").ap()
        filt_dram = nc.dram_tensor("filter_scratch", [GROUPS, P, EG], F32, kind="Internal").ap()

        ident = sb("ident", [P, P])
        wload = sb("wload", [P, 6, D])
        att = sb("att", [P, 3])
        loop_ext = sb("loop_ext", [P, DX])
        src_w = sb("src_w", [P, DX])
        rel_w = sb("rel_w", [P, DX])
        dst_w = sb("dst_w", [P, DX])
        fc1_t = sb("fc1_t", [P, D])
        w1_t = sb("w1_t", [P, D])
        w2_t = sb("w2_t", [P, D])
        b1_col = sb("b1_col", [P, 1])
        cap_b1 = sb("cap_b1", [P, 1])
        b2_row = sb("b2_row", [P, D])
        b2_fold = sb("b2_fold", [P, D])
        minus_log2 = sb("minus_log2", [P, P])

        xdst = sb("xdst", [P, TILES * D])
        score = sb("score", [P, TILES])
        cols = sb("cols", [P, TILES, 3])
        gidx = sb("gidx", [P, GROUPS, 2 * ET], I32)
        sidx = sb("sidx", [P, TILES], I32)

        src_i = sb("src_i", [HALF, 2, P], I32)
        dst_i = sb("dst_i", [HALF, 2, P], I32)
        nxt_i = sb("nxt_i", [HALF, 2, P], I32)
        dst_f = sb("dst_f", [HALF, 2, P])
        row_a = sb("row_a", [HALF, 2, P])
        row_b = sb("row_b", [HALF, 2, P])
        edge_cols = sb("edge_cols", [P, TILES])

        xn = sb("xn", [P, 2, NT, D])
        xs = sb("xs", [P, 2, 2 * ET, D])
        eab = sb("eab", [P, 2, ET, D])
        normed = sb("normed", [P, 2, LT, D])
        hT = sb("hT", [P, 5, EG])
        x1b = sb("x1b", [P, 2, NT, D])
        mg = sb("mg", [P, 2, 2 * ET, DX])
        filt = sb("filt", [P, 2, EG])
        soft = sb("soft", [P, 4, EG])
        stats = sb("stats", [P, 2, LT, 6])
        mv = sb("mv", [P, 2, LT, 2])
        ln_v = sb("ln_v", [P, 2, LT])
        guess = sb("guess", [P, 2, LT])
        newt = sb("newt", [P, 2, LT])
        rstd = sb("rstd", [P, 2, LT])
        nmr = sb("nmr", [P, 2, LT])
        gix = sb("gix", [P, 2, 2 * ET], I32)
        six = sb("six", [P, 2, ET], I32)
        drow = sb("drow", [P, 2, EG], I32)
        colb = sb("colb", [P, 2, ET, 3])
        same = xn[:, :, 0:ET, :]
        carry = xn[:, :, ET:2 * ET, :]
        agg = sb("agg", [P, 2, ET, DX])
        den = sb("den", [P, 2, ET])
        rden = sb("rden", [P, 2, ET])
        zsum = sb("zsum", [P, 2, ET])
        eps_col = sb("eps_col", [P, 1])
        cap_col = sb("cap_col", [P, 1])
        one_col = sb("one_col", [P, 1])
        fresh = normed[0:HALF, 0, 0:2, :]
        fresh_back = normed[0:HALF, 0, 2:4, :]
        fwd = normed[0:HALF, 0, 4:6, :]
        bwd = normed[0:HALF, 0, 6:8, :]
        spread = normed[0:HALF, 0, 8:12, :].rearrange("p (q h) d -> p q h d", q=2)
        zkeep = normed[0:HALF, 0, 12:14, :]
        zmax = sb("zmax", [HALF, 2, 2])
        best = sb("best", [HALF, 1])
        tables = hT[0:HALF, 0:2, 0:2 * TILES]
        pick = hT[0:HALF, 2, 0:2 * TILES]

        bank = [ctx.enter_context(nc.psum_tensor(f"bank{i}", [P, 512], F32)) for i in range(8)]
        TB, PB, NB, WB = bank[0:2], bank[2:4], bank[4:6], bank[6:8]

        s_zero = sem("zeroed")
        s_ident = sem("ident_made")
        s_w = sem("weights_loaded")
        s_rows = sem("edge_rows_loaded")
        s_pads = sem("edge_rows_padded")
        s_pe0 = sem("setup_pe_done")
        s_dv0 = sem("setup_dve_done")
        s_idx = sem("indices_ready")
        s_wready = sem("weights_ready")
        s_consts = sem("constants_set")
        s_lw = sem("setup_copies")

        x_in = sem2("nodes_loaded")
        ea_in = sem2("edge_attr_loaded")
        gathered = sem2("rows_gathered")
        gix_set = sem("gather_index_set")
        kept = sem2("xdst_kept")
        s_stat = sem("stats_done")
        s_mv = sem("moments_done")
        s_guess = sem("rstd_guessed")
        s_lnv = sem("ln_var_done")
        s_newt = sem("newton_steps")
        s_nd = sem("normed_by_dve")
        s_na = sem("normed_by_act")
        s_tp = sem("transposed")
        s_te = sem("transposes_evicted")
        s_mg = sem("mg_products")
        s_mge = sem("mg_evicted")
        s_w1 = sem("filter1_product")
        s_w2 = sem("filter2_product")
        s_sa = sem("softplus_act_steps")
        s_sp1 = sem("filter1_done")
        s_zt = sem("filter2_biased")
        s_sp2 = sem("filter2_done")
        s_nh = sem("node_products")
        s_x1 = sem("nodes_combined")
        s_z = sem("score_steps")
        x1_out = sem2("nodes_stored")
        mg_out = sem2("mg_stored")
        filt_out = sem2("filter_stored")

        s_sm_pe = sem("softmax_pe")
        s_sm_dve = sem("softmax_dve")
        s_sm_act = sem("softmax_act")
        s_cols = sem("softmax_done")

        mg_in = sem2("mg_loaded")
        dr_in = sem2("dst_rows_loaded")
        s_cb = sem("columns_copied")
        s_sel = sem("selections_built")
        s_ag = sem("sums_product")
        s_age = sem("sums_evicted")
        s_den = sem("weights_inverted")
        s_at = sem("attended")
        s_xo = sem("x1_rows_done")
        six_set = sem("scatter_index_set")
        scattered = sem2("x1_scattered")
        kept1 = sem2("x1_kept")

        gathered1 = sem2("x1_gathered")
        gix_set1 = sem("gather_index_set_1")
        filt_in = sem2("filter_loaded")
        dr_in1 = sem2("dst_rows_loaded_1")
        s_stat1 = sem("stats_done_1")
        s_mv1 = sem("moments_done_1")
        s_lnv1 = sem("ln_var_done_1")
        s_guess1 = sem("rstd_guessed_1")
        s_newt1 = sem("newton_steps_1")
        s_n1 = sem("normed_1")
        s_tp1 = sem("transposed_1")
        s_te1 = sem("transposes_evicted_1")
        s_f1 = sem("fc1_product")
        s_msg = sem("messages_done")
        s_cb1 = sem("columns_copied_1")
        s_sel1 = sem("selections_built_1")
        s_ag1 = sem("sums_product_1")
        s_age1 = sem("sums_evicted_1")
        s_add1 = sem("sums_added_1")
        s_buf = sem("rows_buffered")
        six_set1 = sem("scatter_index_set_1")
        put = sem2("out_scattered")

        dst_as_row = dst.rearrange("(a n) -> a n", a=1)

        def edge_base(g):
            return g * EG

        block = ctx.enter_context(nc.Block())

        @block.sync
        def _(sp):
            for n, a in enumerate((w, w_r, loop_w, fc1_w, w1, w2)):
                sp.dma_start(wload[:, n, :], a).then_inc(s_w, 16)
            sp.dma_start(att[:, :], att_w.rearrange("(t p) -> p t", p=P),
                         allow_slow_non_contiguous=True).then_inc(s_w, 16)
            sp.dma_start(b1_col[:, :], b1.rearrange("(p a) -> p a", a=1)).then_inc(s_w, 16)
            sp.dma_start(b2_row[:, :], b2.rearrange("(a n) -> a n", a=1).partition_broadcast(P)).then_inc(s_w, 16)
            sp.wait_ge(s_pads, 3)
            h1 = HALF * P
            full = (TILES - 1) * P
            for tile, a, off, rest in ((src_i, src, 0, REST), (dst_i, dst, 0, REST), (nxt_i, dst, 1, REST - 1)):
                sp.dma_start(tile[:, 0, :], a[off:off + h1].rearrange("(t p) -> t p", p=P)).then_inc(s_rows, 16)
                sp.dma_start(tile[0:HALF - 1, 1, :],
                             a[off + h1:off + full].rearrange("(t p) -> t p", p=P)).then_inc(s_rows, 16)
                sp.dma_start(tile[HALF - 1:HALF, 1, 0:rest],
                             a[off + full:E].rearrange("(a n) -> a n", a=1)).then_inc(s_rows, 16)

            def load(grp):
                g, b, n = grp
                final = isinstance(g, int) and g == GROUPS - 1
                wait_apart(sp, s_x1, 2 * (g - 1))
                start = LAST_NODE if final else g * NG
                sp.dma_start(xn[:, b, :, :].rearrange("p t d -> p (t d)"),
                             x[bass.ds(start, NG), :].rearrange("(p t) d -> p (t d)", p=P)).then_inc(x_in[b], 16)
                wait_apart(sp, s_tp, 5 * (g - 1) - 2)
                wait_apart(sp, s_zero, 1)
                tiles = ET - 1 if final else ET
                sp.dma_start(eab[:, b, 0:tiles, :], ea[bass.ds(edge_base(g), tiles * P), :]
                             .rearrange("(t p) d -> p t d", p=P)).then_inc(ea_in[b], 16)
                if final:
                    sp.dma_start(eab[0:REST, b, ET - 1, :], ea[E - REST:E, :]).then_inc(ea_in[b], 16)

            def store(grp):
                g, b, n = grp
                final = isinstance(g, int) and g == GROUPS - 1
                wait_apart(sp, gathered[b], 16 * 2 * ET * (n + 1))
                sp.dma_start(xdst[:, bass.ds(g * EG, EG)],
                             xs[:, b, ET:2 * ET, :].rearrange("p t d -> p (t d)")).then_inc(kept[b], 16)
                wait_apart(sp, s_x1, 2 * (g + 1))
                start = g * NG
                if final:
                    start = LAST_NODE
                    for c in range(2):
                        sp.wait_ge(x1_out[c], 16 * (GROUPS // 2))
                sp.dma_start(out[bass.ds(start, NG), :].rearrange("(p t) d -> p (t d)", p=P),
                             x1b[:, b, :, :].rearrange("p t d -> p (t d)")).then_inc(x1_out[b], 16)
                wait_apart(sp, s_z, 3 * (g + 1))
                sp.dma_start(mg_dram[g], mg[:, b, :, :].rearrange("p t d -> p (t d)")).then_inc(mg_out[b], 16)
                wait_apart(sp, s_sp2, g + 1)
                sp.dma_start(filt_dram[g], filt[:, b, :]).then_inc(filt_out[b], 16)

            pipelined(sp, GROUPS, load, store)

            for b in range(2):
                sp.wait_ge(mg_out[b], 16 * SLOT_USES[b])

            def dst_rows(grp, done, per, target):
                g, b, n = grp
                final = isinstance(g, int) and g == GROUPS - 1
                count = E - (GROUPS - 1) * EG if final else EG
                wait_apart(sp, done, per * (g - 1))
                sp.dma_start(drow[:, b, 0:count],
                             dst_as_row[:, bass.ds(edge_base(g), count)].partition_broadcast(P)).then_inc(target[b], 16)

            def load_sums(grp):
                g, b, n = grp
                dst_rows(grp, s_sel, 2 * ET, dr_in)
                wait_apart(sp, s_xo, g - 1)
                sp.dma_start(mg[:, b, :, :].rearrange("p t d -> p (t d)"), mg_dram[g]).then_inc(mg_in[b], 16)

            def keep_x1(grp):
                g, b, n = grp
                wait_apart(sp, s_xo, g + 1)
                sp.dma_start(xdst[:, bass.ds(g * EG, EG)],
                             x1b[:, b, 0:ET, :].rearrange("p t d -> p (t d)")).then_inc(kept1[b], 16)

            pipelined(sp, GROUPS, load_sums, keep_x1)

            for b in range(2):
                sp.wait_ge(filt_out[b], 16 * SLOT_USES[b])
            sp.wait_ge(s_sel, 2 * ET * GROUPS)

            def load_filter(grp):
                g, b, n = grp
                dst_rows(grp, s_sel1, 2 * ET, dr_in1)
                wait_apart(sp, s_msg, g - 1)
                sp.dma_start(filt[:, b, :], filt_dram[g]).then_inc(filt_in[b], 16)

            in_turn(sp, GROUPS, load_filter)
            for b in range(2):
                sp.wait_ge(x1_out[b], 16 * SLOT_USES[b])
                sp.wait_ge(put[b], 16 * ET * SLOT_USES[b])

        @block.gpsimd
        def _(pool):
            nc.gpsimd.memset(src_i[:, :, :], 0).then_inc(s_pads, 1)
            nc.gpsimd.memset(dst_i[:, :, :], int(PAD_DST)).then_inc(s_pads, 1)
            nc.gpsimd.memset(nxt_i[:, :, :], int(PAD_DST)).then_inc(s_pads, 1)
            nc.gpsimd.memset(ident[:, :], 0.0).then_inc(s_ident, 1)
            pool.wait_ge(s_ident, 1)
            nc.gpsimd.affine_select(out=ident[:, :], in_=ident[:, :], compare_op=ALU.not_equal, fill=1.0,
                                    base=0, pattern=[[-1, P]], channel_multiplier=1).then_inc(s_ident, 1)
            nc.gpsimd.memset(minus_log2[:, :], -LOG2).then_inc(s_ident, 1)
            nc.gpsimd.memset(eab[:, :, :, :], 0.0).then_inc(s_zero, 1)
            nc.gpsimd.memset(agg[:, :, :, :], 0.0).then_inc(s_zero, 1)
            nc.gpsimd.memset(drow[:, :, :], int(PAD_DST)).then_inc(s_zero, 1)

            pool.wait_ge(s_idx, 1)

            def gather(grp):
                g, b, n = grp
                if not (isinstance(g, int) and g < 2):
                    pool.wait_ge(gathered[b], 16 * 2 * ET * n)
                    pool.wait_ge(kept[b], 16 * n)
                    pool.wait_ge(s_nd, NORM_DVE * (g - 1))
                    wait_apart(pool, s_na, NORM_ACT * (g - 1))
                nc.gpsimd.tensor_copy(gix[:, b, :], gidx[:, bass.ds(g, 1), :]
                                      .rearrange("p a t -> p (a t)")).then_inc(gix_set, 1)
                wait_apart(pool, gix_set, g + 1)
                for t in range(2 * ET):
                    pool.indirect_dma_start(xs[:, b, t, :], None, x,
                                            bass.IndirectOffsetOnAxis(gix[:, b, t:t + 1], 0)).then_inc(gathered[b], 16)

            in_turn(pool, GROUPS, gather)

            for b in range(2):
                pool.wait_ge(x1_out[b], 16 * SLOT_USES[b])

            def scatter(grp, done, index_set, data):
                g, b, n = grp
                if not (isinstance(g, int) and g < 2):
                    wait_apart(pool, done[b], 16 * ET * n)
                nc.gpsimd.tensor_copy(six[:, b, :], sidx[:, bass.ds(g * ET, ET)]).then_inc(index_set, 1)
                pool.wait_ge(index_set, g + 1)
                wait_apart(pool, data, g + 1)
                for t in range(ET):
                    pool.indirect_dma_start(out, bass.IndirectOffsetOnAxis(six[:, b, t:t + 1], 0), x1b[:, b, t, :],
                                            None, bounds_check=N - 1, oob_is_err=False).then_inc(done[b], 16)

            in_turn(pool, GROUPS, lambda grp: scatter(grp, scattered, six_set, s_xo))

            for b in range(2):
                pool.wait_ge(scattered[b], 16 * ET * SLOT_USES[b])

            def gather_again(grp):
                g, b, n = grp
                if not (isinstance(g, int) and g < 2):
                    pool.wait_ge(gathered1[b], 16 * ET * n)
                    wait_apart(pool, s_n1, ET * (g - 1))
                nc.gpsimd.tensor_copy(gix[:, b, 0:ET], gidx[:, bass.ds(g, 1), 0:ET]
                                      .rearrange("p a t -> p (a t)")).then_inc(gix_set1, 1)
                wait_apart(pool, gix_set1, g + 1)
                for t in range(ET):
                    pool.indirect_dma_start(xs[:, b, t, :], None, out,
                                            bass.IndirectOffsetOnAxis(gix[:, b, t:t + 1], 0)).then_inc(gathered1[b], 16)

            in_turn(pool, GROUPS, gather_again)

            for b in range(2):
                pool.wait_ge(gathered1[b], 16 * ET * SLOT_USES[b])
            in_turn(pool, GROUPS, lambda grp: scatter(grp, put, six_set1, s_buf))
            for b in range(2):
                pool.wait_ge(put[b], 16 * ET * SLOT_USES[b])

        @block.tensor
        def _(pe):
            pe.wait_ge(s_ident, 3)
            pe.wait_ge(s_w, 16 * 9)
            for n, i in enumerate((0, 1, 3, 4)):
                last = pe.transpose(bank[0][:, n * D:(n + 1) * D], wload[:, i, :], ident[:, :])
            last.then_inc(s_pe0, 1)
            pe.transpose(bank[1][:, 0:D], wload[:, 5, :], ident[:, :]).then_inc(s_pe0, 1)
            pe.wait_ge(s_dv0, 1)
            pe.matmul(bank[2][:, 0:DX], wload[:, 0, :], loop_ext[:, :], start=True, stop=True)
            pe.matmul(bank[2][:, 256:257], wload[:, 0, :], att[:, 0:1], start=True, stop=True)
            pe.matmul(bank[2][:, 260:261], wload[:, 1, :], att[:, 2:3], start=True, stop=True).then_inc(s_pe0, 1)
            pe.wait_ge(s_dv0, 3)
            pe.matmul(bank[3][:, 0:D], minus_log2[:, :], w2_t[:, :], start=True, stop=True).then_inc(s_pe0, 1)
            for q in range(4):
                pe.wait_ge(s_dv0, 6 + 2 * q)
                for h in range(2):
                    last = pe.transpose(bank[4][:, h * HALF:(h + 1) * HALF],
                                        (row_a if q < 3 else dst_f)[:, h, :], ident[0:HALF, 0:HALF])
                last.then_inc(s_pe0, 1)

            pe.wait_ge(s_wready, 1)

            def transposes(grp, i, source, psum):
                g, b, n = grp
                q = 5 * g + i
                wait(pe, s_te, q - 1)
                for t in range(ET):
                    last = pe.transpose(psum[:, t * P:(t + 1) * P], source(t), ident[:, :])
                last.then_inc(s_tp, 1)

            def edges_and_nodes(grp):
                g, b, n = grp

                def nrm(k):
                    return lambda t: normed[:, b, k + t, :]

                def pair(i, lo, r):
                    wait(pe, s_mge, 4 * g + r - 1)
                    psum = PB[r % 2]
                    for t in range(lo, lo + 2):
                        o = psum[:, (t - lo) * DX:(t - lo + 1) * DX]
                        tile = slice(t * P, (t + 1) * P)
                        if r % 2 == 0:
                            last = pe.matmul(o, hT[:, 1, tile], dst_w[:, :], start=True, stop=True)
                        else:
                            pe.matmul(o, hT[:, 0, tile], src_w[:, :], start=True, stop=False)
                            last = pe.matmul(o, hT[:, 2, tile], rel_w[:, :], start=False, stop=True)
                    last.then_inc(s_mg, 1)

                def node_half(half):
                    pe.wait_ge(s_te, 5 * g + 4 + half)
                    wait(pe, s_x1, 2 * g - 1 + half)
                    for t in range(4):
                        last = pe.matmul(NB[half][:, t * D:(t + 1) * D], hT[:, 3 + half, t * P:(t + 1) * P],
                                         src_w[:, 0:D], start=True, stop=True)
                    last.then_inc(s_nh, 1)

                pe.wait_ge(s_nd, NORM_DVE * (g + 1))
                pe.wait_ge(s_na, NORM_ACT * (g + 1))
                transposes(grp, 0, nrm(NT), TB[b])
                transposes(grp, 1, nrm(NT + ET), TB[1 - b])
                pe.wait_ge(ea_in[b], 16 * (n + 1) + (16 if isinstance(g, int) and g == GROUPS - 1 else 0))
                transposes(grp, 2, lambda t: eab[:, b, t, :], TB[b])
                transposes(grp, 3, nrm(0), TB[1 - b])
                pe.wait_ge(s_te, 5 * g + 2)
                pair(0, 0, 0)
                pe.wait_ge(s_te, 5 * g + 3)
                wait(pe, s_sp1, g)
                pe.matmul(WB[0][:, :], w1_t[:, :], hT[:, 2, :], start=True, stop=True).then_inc(s_w1, 1)
                pair(1, 0, 1)
                transposes(grp, 4, nrm(4), TB[b])
                pair(2, 2, 2)
                node_half(0)
                pair(3, 2, 3)
                node_half(1)
                pe.wait_ge(s_sp1, g + 1)
                wait(pe, s_zt, g)
                for t in range(ET):
                    last = pe.matmul(WB[1][:, t * D:(t + 1) * D], soft[:, 2, t * P:(t + 1) * P], w2_t[:, :],
                                     start=True, stop=True)
                last.then_inc(s_w2, 1)

            in_turn(pe, GROUPS, edges_and_nodes)

            pe.wait_ge(s_z, 3 * GROUPS)
            pe.wait_ge(s_te, 5 * GROUPS)
            for h in range(2):
                last = pe.transpose(bank[0][0:HALF, h * P:(h + 1) * P], score[:, h * HALF:(h + 1) * HALF], ident[:, :])
            last.then_inc(s_sm_pe, 1)
            for q in range(4):
                pe.wait_ge(s_sm_dve, SM_BCAST + q)
                for h in range(2):
                    last = pe.transpose(bank[1 + q // 2][:, (q % 2) * TILES + h * HALF:(q % 2) * TILES + (h + 1) * HALF],
                                        spread[:, q % 2, h, :], ident[0:HALF, 0:HALF])
                last.then_inc(s_sm_pe, 1)
            pe.wait_ge(s_sm_act, 1)
            for h in range(2):
                last = pe.transpose(bank[3][:, h * HALF:(h + 1) * HALF], row_b[:, h, :], ident[0:HALF, 0:HALF])
            last.then_inc(s_sm_pe, 1)

            def sums(grp, count, rows, width, selected, evicted, used):
                g, b, n = grp

                def own(j):
                    pe.wait_ge(selected, 2 * ET * g + 2 * j + 2)
                    wait(pe, evicted, count * g + j - ET + 1)
                    pe.matmul(bank[j][:, 0:width], same[:, b, j, :], rows(j), start=True, stop=False)

                own(0)
                for j in range(ET):
                    if j + 1 < ET:
                        own(j + 1)
                    wait(pe, evicted, count * g + j)
                    before = agg[:, b, j - 1, 0:width] if j else agg[:, 1 - b, ET - 1, 0:width]
                    pe.matmul(bank[j][:, 0:width], carry[:, b, j, :], before, start=False, stop=True).then_inc(used, 1)

            def attend(grp):
                g, b, n = grp
                pe.wait_ge(mg_in[b], 16 * (n + 1))
                sums(grp, ET, lambda j: mg[:, b, j, :], DX, s_sel, s_age, s_ag)

            pe.wait_ge(s_cols, 1)
            pe.wait_ge(s_zero, 3)
            in_turn(pe, GROUPS, attend)

            pe.wait_ge(s_den, 2 * GROUPS)

            def project(grp):
                g, b, n = grp
                pe.wait_ge(s_n1, ET * (g + 1))
                wait(pe, s_te1, g)
                for t in range(ET):
                    last = pe.transpose(bank[4][:, t * P:(t + 1) * P], normed[:, b, t, :], ident[:, :])
                last.then_inc(s_tp1, 1)
                pe.wait_ge(s_te1, g + 1)
                wait(pe, s_msg, g)
                for t in range(ET):
                    last = pe.matmul(bank[5][:, t * D:(t + 1) * D], hT[:, 0, t * P:(t + 1) * P], fc1_t[:, :],
                                     start=True, stop=True)
                last.then_inc(s_f1, 1)

            def convolve(grp):
                g, b, n = grp
                pe.wait_ge(s_msg, g + 1)
                sums(grp, ET, lambda j: x1b[:, b, ET + j, :], D, s_sel1, s_age1, s_ag1)

            pipelined(pe, GROUPS, project, convolve)

        @block.scalar
        def _(act):
            act.preload_act_table_set("natural_log_exp_and_others")

            def guess_rstd(grp, moments, ln_done, guessed, lt):
                g, b, n = grp
                act.wait_ge(moments, lt * (g + 1))
                wait(act, guessed, g)
                act.activation(ln_v[:, b, 0:lt], mv[:, b, 0:lt, 1], ACT.Ln, bias=eps_col[:, 0:1]).then_inc(ln_done, 1)
                act.wait_ge(ln_done, g + 1)
                act.activation(guess[:, b, 0:lt], ln_v[:, b, 0:lt], ACT.Exp, scale=-0.5).then_inc(guessed, 1)

            def normalize(grp):
                g, b, n = grp
                act.wait_ge(s_newt, 5 * (g + 1))
                wait(act, s_tp, 5 * (g - 1))
                for t in range(NORM_ACT):
                    act.activation(normed[:, b, t, :], xn[:, b, t, :] if t < NT else xs[:, b, t - NT, :], ACT.Identity,
                                   bias=nmr[:, b, t:t + 1], scale=rstd[:, b, t:t + 1]).then_inc(s_na, 1)

            def evict(grp, i, psum, func):
                g, b, n = grp
                act.wait_ge(s_tp, 5 * g + i + 1)
                if i < 3:
                    wait(act, s_mg, 4 * g)
                else:
                    wait(act, s_nh, 2 * g - 4 + i)
                act.activation(hT[:, i, :], psum[:, :], func).then_inc(s_te, 1)

            def evict_pair(grp, r):
                g, b, n = grp
                act.wait_ge(s_mg, 4 * g + r + 1)
                if r == 0 and not (isinstance(g, int) and g < 2):
                    act.wait_ge(mg_out[b], 16 * n)
                lo = (r // 2) * 2 + (ET if r % 2 == 0 else 0)
                act.copy(mg[:, b, lo:lo + 2, :].rearrange("p t d -> p (t d)"), PB[r % 2][:, 0:2 * DX]).then_inc(s_mge, 1)

            def softplus_steps(g, k, source, bias):
                wait(act, s_sa, 6 * g + k)
                act.activation(soft[:, 0, :], source, ACT.Relu, scale=-1.0, bias=bias).then_inc(s_sa, 1)
                act.wait_ge(s_sa, 6 * g + k + 1)
                act.activation(soft[:, 0, :], soft[:, 0, :], ACT.Exp, scale=-1.0, bias=cap_col[:, 0:1]).then_inc(s_sa, 1)
                act.wait_ge(s_sa, 6 * g + k + 2)
                wait(act, s_sp2 if k == 0 else s_sp1, g if k == 0 else g + 1)
                act.activation(soft[:, 1, :], soft[:, 0, :], ACT.Ln, bias=one_col[:, 0:1]).then_inc(s_sa, 1)

            def ahead(grp):
                guess_rstd(grp, s_mv, s_lnv, s_guess, LT)

            def first_half(grp):
                g, b, n = grp
                evict(grp, 0, TB[b], ACT.Relu)
                evict(grp, 1, TB[1 - b], ACT.Relu)
                evict(grp, 2, TB[b], ACT.Copy)
                evict(grp, 3, TB[1 - b], ACT.Relu)
                evict_pair(grp, 0)
                act.wait_ge(s_w1, g + 1)
                softplus_steps(g, 0, WB[0][:, :], cap_b1[:, 0:1])
                evict_pair(grp, 1)
                evict(grp, 4, TB[b], ACT.Relu)

            def second_half(grp):
                g, b, n = grp
                evict_pair(grp, 2)
                evict_pair(grp, 3)
                act.wait_ge(s_zt, g + 1)
                softplus_steps(g, 3, soft[:, 3, :], cap_col[:, 0:1])

            act.wait_ge(s_wready, 1)
            g0, g1 = (0, 0, 0), (1, 1, 0)
            ahead(g0)
            normalize(g0)

            def step(grp, nxt):
                first_half(grp)
                ahead(nxt)
                second_half(grp)
                normalize(nxt)

            step(g0, g1)
            with act.Fori(0, (GROUPS - 3) // 2) as k:
                step((2 * k + 1, 1, k), (2 * k + 2, 0, k + 1))
                step((2 * k + 2, 0, k + 1), (2 * k + 3, 1, k + 1))
            L = GROUPS - 1
            step((L - 1, 1, L // 2 - 1), (L, 0, L // 2))
            first_half((L, 0, L // 2))
            second_half((L, 0, L // 2))

            act.wait_ge(s_sm_dve, SM_SHIFTED)
            act.activation(row_b[:, :, :], row_a[:, :, :], ACT.Exp).then_inc(s_sm_act, 1)

            def evict_sums(grp, width, ready, evicted, used, per):
                g, b, n = grp
                for j in range(ET):
                    act.wait_ge(ready, ET * g + j + 1)
                    if j == 0:
                        wait(act, used, per * (g - 1))
                    act.copy(agg[:, b, j, 0:width], bank[j][:, 0:width]).then_inc(evicted, 1)

            act.wait_ge(s_zero, 3)
            in_turn(act, GROUPS, lambda grp: evict_sums(grp, DX, s_ag, s_age, s_at, ET))

            def ahead1(grp):
                g, b, n = grp
                guess_rstd(grp, s_mv1, s_lnv1, s_guess1, ET)

            def normalize1(grp):
                g, b, n = grp
                act.wait_ge(s_newt1, 5 * (g + 1))
                wait(act, s_tp1, g - 1)
                for t in range(ET):
                    act.activation(normed[:, b, t, :], xs[:, b, t, :], ACT.Identity,
                                   bias=nmr[:, b, t:t + 1], scale=rstd[:, b, t:t + 1]).then_inc(s_n1, 1)
                act.wait_ge(s_tp1, g + 1)
                wait(act, s_f1, g)
                act.activation(hT[:, 0, :], bank[4][:, :], ACT.Relu).then_inc(s_te1, 1)

            def first1(grp):
                ahead1(grp)
                normalize1(grp)

            act.wait_ge(s_at, ET * GROUPS)
            pipelined(act, GROUPS, first1, lambda grp: evict_sums(grp, D, s_ag1, s_age1, s_add1, 1))

            def buffer_rows(grp):
                g, b, n = grp
                if not (isinstance(g, int) and g < 2):
                    act.wait_ge(put[b], 16 * ET * n)
                act.copy(x1b[:, b, 0:ET, :].rearrange("p t d -> p (t d)"),
                         xdst[:, bass.ds(g * EG, EG)]).then_inc(s_buf, 1)

            act.wait_ge(s_add1, GROUPS)
            act.wait_ge(scattered[0], 16 * ET * SLOT_USES[0])
            act.wait_ge(scattered[1], 16 * ET * SLOT_USES[1])
            in_turn(act, GROUPS, buffer_rows)

        @block.vector
        def _(dve):
            v = nc.vector
            done = [0]

            def setup(ins):
                done[0] += 1
                ins.then_inc(s_dv0, 1)
                dve.wait_ge(s_dv0, done[0])

            v.memset(eps_col[:, :], EPS).then_inc(s_consts, 1)
            v.memset(cap_col[:, :], CAP).then_inc(s_consts, 1)
            v.memset(one_col[:, :], 1.0).then_inc(s_consts, 1)
            dve.wait_ge(s_consts, 3)
            dve.wait_ge(s_w, 16 * 9)
            v.tensor_copy(loop_ext[:, 0:D], wload[:, 2, :]).then_inc(s_lw, 1)
            setup(v.tensor_copy(loop_ext[:, D:DX], att[:, 1:2]))
            setup(v.tensor_scalar(cap_b1[:, :], b1_col[:, :], -1.0, CAP, ALU.mult, ALU.add))
            dve.wait_ge(s_pe0, 2)
            setup(v.tensor_copy(w2_t[:, :], bank[1][:, 0:D]))
            for n, dest in enumerate((src_w, rel_w, fc1_t, w1_t)):
                v.tensor_copy(dest[:, 0:D], bank[0][:, n * D:(n + 1) * D]).then_inc(s_lw, 1)
            dve.wait_ge(s_pe0, 3)
            v.tensor_copy(dst_w[:, :], bank[2][:, 0:DX]).then_inc(s_lw, 1)
            v.tensor_copy(src_w[:, D:DX], bank[2][:, 256:257]).then_inc(s_lw, 1)
            v.tensor_copy(rel_w[:, D:DX], bank[2][:, 260:261]).then_inc(s_lw, 1)
            dve.wait_ge(s_pe0, 4)
            v.tensor_tensor(b2_fold[:, :], bank[3][:, 0:D], b2_row[:, :], ALU.add).then_inc(s_lw, 1)
            dve.wait_ge(s_lw, 9)
            dve.wait_ge(s_rows, 16 * 9)
            setup(v.tensor_copy(dst_f[:, :, :], dst_i[:, :, :]))
            setup(v.tensor_copy(row_b[:, :, :], nxt_i[:, :, :]))
            setup(v.tensor_copy(row_a[:, :, :], src_i[:, :, :]))
            grouped = [bank[4][:, 0:TILES].rearrange("p (g t) -> p g t", t=ET)]
            dve.wait_ge(s_pe0, 5)
            setup(v.tensor_copy(gidx[:, :, 0:ET], grouped[0]))
            setup(v.tensor_scalar(row_a[:, :, :], dst_f[:, :, :], float(N - 1), None, ALU.min))
            dve.wait_ge(s_pe0, 6)
            setup(v.tensor_copy(gidx[:, :, ET:2 * ET], grouped[0]))
            v.tensor_tensor(row_b[:, :, :], dst_f[:, :, :], row_b[:, :, :], ALU.is_equal).then_inc(s_lw, 1)
            dve.wait_ge(s_lw, 10)
            setup(v.scalar_tensor_tensor(out=row_a[:, :, :], in0=row_b[:, :, :], scalar=SKIP, in1=dst_f[:, :, :],
                                         op0=ALU.mult, op1=ALU.add))
            dve.wait_ge(s_pe0, 7)
            setup(v.tensor_copy(sidx[:, :], bank[4][:, 0:TILES]))
            setup(v.memset(cols[:, 0:1, 2], -1.0))
            dve.wait_ge(s_pe0, 8)
            v.tensor_copy(edge_cols[:, :], bank[4][:, 0:TILES]).then_inc(s_lw, 1)
            dve.wait_ge(s_lw, 11)
            v.tensor_copy(cols[:, :, 0], edge_cols[:, :]).then_inc(s_lw, 1)
            v.tensor_scalar(cols[:, 1:TILES, 2], edge_cols[:, 0:TILES - 1], 1.0, ident[:, P - 1:P],
                            ALU.add, ALU.mult).then_inc(s_lw, 1)
            dve.wait_ge(s_lw, 13)
            v.tensor_scalar(cols[:, 1:TILES, 2], cols[:, 1:TILES, 2], -1.0, None, ALU.add).then_inc(s_lw, 1)
            dve.wait_ge(s_lw, 14)
            v.memset(den[:, :, :], 1.0).then_inc(s_idx, 1)
            dve.wait_ge(s_idx, 1)
            v.memset(rden[:, :, :], 1.0).then_inc(s_wready, 1)

            def moments(grp, stat, mom, lt, tile):
                g, b, n = grp
                for t in range(lt):
                    tile(t)
                for t in range(lt):
                    wait_apart(dve, stat, lt * g + t + 1)
                    v.bn_aggr(mv[:, b, t, :], stats[:, b, t, :]).then_inc(mom, 1)

            def newton(grp, guessed, steps, mom, lt):
                g, b, n = grp
                y, u = guess[:, b, 0:lt], newt[:, b, 0:lt]
                dve.wait_ge(guessed, g + 1)
                v.tensor_tensor(u, y, y, ALU.mult).then_inc(steps, 1)
                dve.wait_ge(steps, 5 * g + 1)
                dve.wait_ge(mom, lt * (g + 1))
                v.scalar_tensor_tensor(out=u, in0=mv[:, b, 0:lt, 1], scalar=EPS, in1=u,
                                       op0=ALU.add, op1=ALU.mult).then_inc(steps, 1)
                dve.wait_ge(steps, 5 * g + 2)
                v.tensor_scalar(u, u, -0.5, 1.5, ALU.mult, ALU.add).then_inc(steps, 1)
                dve.wait_ge(steps, 5 * g + 3)
                v.tensor_tensor(rstd[:, b, 0:lt], y, u, ALU.mult).then_inc(steps, 1)
                dve.wait_ge(steps, 5 * g + 4)
                v.scalar_tensor_tensor(out=nmr[:, b, 0:lt], in0=mv[:, b, 0:lt, 0], scalar=-1.0,
                                       in1=rstd[:, b, 0:lt], op0=ALU.mult, op1=ALU.mult).then_inc(steps, 1)

            def ahead(grp):
                g, b, n = grp
                dve.wait_ge(x_in[b], 16 * (n + 1))

                def tile(t):
                    if t == NT:
                        dve.wait_ge(gathered[b], 16 * 2 * ET * (n + 1))
                    v.bn_stats(stats[:, b, t, :], xn[:, b, t, :] if t < NT else xs[:, b, t - NT, :]).then_inc(s_stat, 1)

                moments(grp, s_stat, s_mv, LT, tile)

            def normalize(grp):
                g, b, n = grp
                newton(grp, s_guess, s_newt, s_mv, LT)
                wait(dve, s_tp, 5 * (g - 1))
                dve.wait_ge(s_newt, 5 * g + 4)
                for t in range(NORM_ACT, LT):
                    v.tensor_scalar(normed[:, b, t, :], xn[:, b, t, :] if t < NT else xs[:, b, t - NT, :],
                                    mv[:, b, t, 0:1], rstd[:, b, t:t + 1], ALU.subtract, ALU.mult).then_inc(s_nd, 1)

            def first_filter(grp):
                g, b, n = grp
                dve.wait_ge(s_sa, 6 * g + 3)
                wait(dve, s_w2, g)
                v.scalar_tensor_tensor(out=soft[:, 2, :], in0=WB[0][:, :], scalar=b1_col[:, 0:1], in1=soft[:, 1, :],
                                       op0=ALU.add, op1=ALU.max).then_inc(s_sp1, 1)

            def second_half(grp):
                g, b, n = grp
                for half in range(2):
                    dve.wait_ge(s_nh, 2 * g + half + 1)
                    if half == 0 and not (isinstance(g, int) and g < 2):
                        dve.wait_ge(x1_out[b], 16 * n)
                    rows = slice(4 * half, 4 * half + 4)
                    v.scalar_tensor_tensor(out=x1b[:, b, rows, :].rearrange("p t d -> p (t d)"), in0=NB[half][:, :],
                                           scalar=0.0, in1=xn[:, b, rows, :].rearrange("p t d -> p (t d)"),
                                           op0=ALU.max, op1=ALU.add).then_inc(s_x1, 1)
                dve.wait_ge(s_w2, g + 1)
                wait(dve, s_sp2, g)
                v.scalar_tensor_tensor(out=soft[:, 3, :].rearrange("p (t d) -> p t d", d=D),
                                       in0=WB[1][:, :].rearrange("p (t d) -> p t d", d=D), scalar=1.0,
                                       in1=b2_fold[:, :].unsqueeze(1).broadcast_to([P, ET, D]),
                                       op0=ALU.mult, op1=ALU.add).then_inc(s_zt, 1)
                dve.wait_ge(s_mge, 4 * (g + 1))
                v.tensor_tensor(zsum[:, b, :], mg[:, b, 0:ET, D], mg[:, b, ET:2 * ET, D], ALU.add).then_inc(s_z, 1)
                dve.wait_ge(s_z, 3 * g + 1)
                v.scalar_tensor_tensor(out=score[:, bass.ds(g * ET, ET)], in0=zsum[:, b, :], scalar=0.01,
                                       in1=zsum[:, b, :], op0=ALU.mult, op1=ALU.max).then_inc(s_z, 1)
                v.memset(mg[:, b, 0:ET, D], 1.0).then_inc(s_z, 1)
                dve.wait_ge(s_sa, 6 * g + 6)
                dve.wait_ge(s_zt, g + 1)
                if not (isinstance(g, int) and g < 2):
                    dve.wait_ge(filt_out[b], 16 * n)
                v.tensor_tensor(filt[:, b, :], soft[:, 3, :], soft[:, 1, :], ALU.max).then_inc(s_sp2, 1)

            g0, g1 = (0, 0, 0), (1, 1, 0)
            ahead(g0)
            normalize(g0)

            def step(grp, nxt):
                ahead(nxt)
                first_filter(grp)
                normalize(nxt)
                second_half(grp)

            step(g0, g1)
            with dve.Fori(0, (GROUPS - 3) // 2) as k:
                step((2 * k + 1, 1, k), (2 * k + 2, 0, k + 1))
                step((2 * k + 2, 0, k + 1), (2 * k + 3, 1, k + 1))
            L = GROUPS - 1
            step((L - 1, 1, L // 2 - 1), (L, 0, L // 2))
            first_filter((L, 0, L // 2))
            second_half((L, 0, L // 2))

            count = [0]

            def sm(ins):
                count[0] += 1
                ins.then_inc(s_sm_dve, 1)
                dve.wait_ge(s_sm_dve, count[0])

            flat = "p h e -> p (h e)"
            dve.wait_ge(s_sm_pe, 1)
            zr = row_a
            sm(v.tensor_copy(zr[:, :, :].rearrange(flat), bank[0][0:HALF, 0:2 * P]))
            sm(v.memset(fresh[:, :, :], -FAR))
            sm(v.tensor_tensor(fresh[:, :, 1:P], dst_f[:, :, 1:P], dst_f[:, :, 0:P - 1], ALU.not_equal))
            sm(v.tensor_scalar(fresh[:, :, 1:P], fresh[:, :, 1:P], -FAR, None, ALU.mult))
            sm(v.memset(fresh_back[:, :, :], -FAR))
            sm(v.tensor_copy(fresh_back[:, :, 0:P - 1], fresh[:, :, 1:P]))

            def run_max(forward, backward):
                a, z = fresh[:, :, :].rearrange(flat), zr[:, :, :].rearrange(flat)
                ab = fresh_back[:, :, :].rearrange(flat)
                sm(v.tensor_tensor_scan(forward[:, :, :].rearrange(flat), a, z, -FAR, ALU.add, ALU.max))
                sm(v.tensor_tensor_scan(backward[:, :, :].rearrange(flat)[:, ::-1], ab[:, ::-1], z[:, ::-1], -FAR,
                                        ALU.add, ALU.max))

            run_max(fwd, bwd)
            assert count[0] == 8
            for q, (column, source) in enumerate(((P - 1, dst_f), (0, dst_f), (P - 1, fwd), (0, bwd))):
                if q >= 2:
                    dve.wait_ge(s_sm_pe, q)
                sm(v.tensor_copy(spread[:, q % 2, :, :], source[:, :, column:column + 1].broadcast_to([HALF, 2, P])))
            dve.wait_ge(s_sm_pe, 5)
            sm(v.tensor_copy(tables[:, 0, :], bank[1][0:HALF, 0:2 * TILES]))
            sm(v.tensor_copy(tables[:, 1, :], bank[2][0:HALF, 0:2 * TILES]))
            for h in range(2):
                for column in (0, P - 1):
                    sm(v.tensor_scalar(pick[:, :], tables[:, 0, :], dst_f[:, h, column:column + 1], -FAR,
                                       ALU.not_equal, ALU.mult))
                    sm(v.tensor_tensor(pick[:, :], pick[:, :], tables[:, 1, :], ALU.add))
                    sm(v.tensor_reduce(best[:, :], pick[:, :], AX.X, ALU.max))
                    sm(v.tensor_tensor(zmax[:, h, (0 if column == 0 else 1):(1 if column == 0 else 2)],
                                       zr[:, h, column:column + 1], best[:, :], ALU.max))
            sm(v.tensor_copy(zkeep[:, :, :], zr[:, :, :]))
            sm(v.tensor_copy(zr[:, :, 0:1], zmax[:, :, 0:1]))
            sm(v.tensor_copy(zr[:, :, P - 1:P], zmax[:, :, 1:2]))
            run_max(fwd, bwd)
            sm(v.tensor_tensor(fwd[:, :, :], fwd[:, :, :], bwd[:, :, :], ALU.max))
            sm(v.tensor_tensor(row_a[:, :, :], zkeep[:, :, :], fwd[:, :, :], ALU.subtract))
            assert count[0] == SM_SHIFTED
            dve.wait_ge(s_sm_pe, 6)
            v.tensor_copy(cols[:, :, 1], bank[3][:, 0:TILES]).then_inc(s_cols, 1)
            dve.wait_ge(s_cols, 1)

            def selections(grp, rows_in, copied, built, used, weighted):
                g, b, n = grp
                wait(dve, used, ET * (g - 1))
                v.tensor_copy(colb[:, b, :, :], cols[:, bass.ds(g * ET, ET), :]).then_inc(copied, 1)
                dve.wait_ge(copied, g + 1)
                dve.wait_ge(rows_in[b], 16 * (n + 1))
                for j in range(ET):
                    row = drow[:, b, j * P:(j + 1) * P]
                    if weighted:
                        v.tensor_scalar(same[:, b, j, :], row, colb[:, b, j, 0:1], colb[:, b, j, 1:2],
                                        ALU.is_equal, ALU.mult).then_inc(built, 1)
                    else:
                        v.tensor_scalar(same[:, b, j, :], row, colb[:, b, j, 0:1], None,
                                        ALU.is_equal).then_inc(built, 1)
                    v.tensor_scalar(carry[:, b, j, :], row, colb[:, b, j, 2:3], None,
                                    ALU.is_equal).then_inc(built, 1)

            def select(grp):
                selections(grp, dr_in, s_cb, s_sel, s_ag, True)

            def finish_x1(grp):
                g, b, n = grp
                dve.wait_ge(s_age, ET * (g + 1))
                v.tensor_scalar(den[:, b, :], agg[:, b, :, D], 1e-30, None, ALU.max).then_inc(s_den, 1)
                dve.wait_ge(s_den, 2 * g + 1)
                v.reciprocal(rden[:, b, :], den[:, b, :]).then_inc(s_den, 1)
                dve.wait_ge(s_den, 2 * g + 2)
                for j in range(ET):
                    v.scalar_tensor_tensor(out=normed[:, b, j, :], in0=agg[:, b, j, 0:D], scalar=rden[:, b, j:j + 1],
                                           in1=mg[:, b, ET + j, 0:D], op0=ALU.mult, op1=ALU.add).then_inc(s_at, 1)
                dve.wait_ge(s_at, ET * (g + 1))
                if not (isinstance(g, int) and g < 2):
                    dve.wait_ge(scattered[b], 16 * ET * n)
                    dve.wait_ge(kept1[b], 16 * n)
                v.scalar_tensor_tensor(out=x1b[:, b, 0:ET, :].rearrange("p t d -> p (t d)"),
                                       in0=normed[:, b, 0:ET, :].rearrange("p t d -> p (t d)"), scalar=0.0,
                                       in1=xdst[:, bass.ds(g * EG, EG)], op0=ALU.max, op1=ALU.add).then_inc(s_xo, 1)

            for b in range(2):
                dve.wait_ge(kept[b], 16 * SLOT_USES[b])
                dve.wait_ge(x1_out[b], 16 * SLOT_USES[b])
            for b in range(2):
                dve.wait_ge(mg_in[b], 16)
            dve.wait_ge(s_zero, 3)
            pipelined(dve, GROUPS, select, finish_x1)

            for b in range(2):
                dve.wait_ge(kept1[b], 16 * SLOT_USES[b])

            def ahead1(grp):
                g, b, n = grp
                dve.wait_ge(gathered1[b], 16 * ET * (n + 1))
                moments(grp, s_stat1, s_mv1, ET,
                        lambda t: v.bn_stats(stats[:, b, t, :], xs[:, b, t, :]).then_inc(s_stat1, 1))
                selections(grp, dr_in1, s_cb1, s_sel1, s_ag1, False)
                newton(grp, s_guess1, s_newt1, s_mv1, ET)

            def messages(grp):
                g, b, n = grp
                dve.wait_ge(s_f1, g + 1)
                dve.wait_ge(filt_in[b], 16 * (n + 1))
                wait(dve, s_ag1, ET * (g - 1))
                v.scalar_tensor_tensor(out=x1b[:, b, ET:2 * ET, :].rearrange("p t d -> p (t d)"), in0=filt[:, b, :],
                                       scalar=-LOG2, in1=bank[5][:, :], op0=ALU.add, op1=ALU.mult).then_inc(s_msg, 1)

            def add_sums(grp):
                g, b, n = grp
                dve.wait_ge(s_age1, ET * (g + 1))
                here = xdst[:, bass.ds(g * EG, EG)].rearrange("p (t d) -> p t d", d=D)
                v.tensor_tensor(here, here, agg[:, b, :, 0:D], ALU.add).then_inc(s_add1, 1)

            def second1(grp):
                messages(grp)
                add_sums(grp)

            pipelined(dve, GROUPS, ahead1, second1)


_INS = ["x", "src", "dst", "edge_attr_128", "L0_gnn_w", "L0_gnn_w_r", "L0_gnn_att_w", "L0_gnn_loop_w",
        "L1_gnn_fc1_w", "L1_gnn_w1", "L1_gnn_b1", "L1_gnn_w2", "L1_gnn_b2"]


def kernel(**inputs):
    import concourse.bacc as bacc
    import numpy as np
    from concourse.bass_utils import run_bass_kernel_spmd

    nc = bacc.Bacc("TRN2", target_bir_lowering=False, num_devices=1)
    arrays, args = {}, []
    for name in _INS:
        a = np.ascontiguousarray(inputs[name])
        arrays[f"in_{name}"] = a
        args.append(nc.dram_tensor(f"in_{name}", a.shape, mybir.dt.from_np(a.dtype), kind="ExternalInput").ap())
    out = nc.dram_tensor("out_x", inputs["x"].shape, F32, kind="ExternalOutput").ap()
    gnn_kernel(nc, *args, out)
    result = run_bass_kernel_spmd(nc, [arrays], core_ids=[0])
    return result.results[0]["out_x"]
```

```python
from contextlib import ExitStack

import concourse.bass as bass
from concourse import mybir

ALU = mybir.AluOpType
ACT = mybir.ActivationFunctionType
AX = mybir.AxisListType
F32 = mybir.dt.float32
I32 = mybir.dt.int32

P = 128
D = 128
DX = D + 1
ET = 4
NT = 8
LT = 2 * ET + NT
EPS = 1e-5
LOG2 = 0.6931471805599453
CAP = 40.0
FAR = 1e30
PAD_DST = 60000.0
NORM_ACT = 7
NORM_DVE = LT - NORM_ACT
SM_BCAST = 9
SM_SHIFTED = 8 + 4 + 2 + 16 + 3 + 2 + 2
SKIP = 100000.0


def wait(eng, sem, value):
    if not (isinstance(value, int) and value <= 0):
        eng.wait_ge(sem, value)


def wait_apart(eng, sem, value):
    wait(eng, sem, value)
    if not isinstance(value, int):
        eng.nop(nofuse=True)


def staged(eng, groups, first, last, step):
    def of(k, c):
        def at(d):
            number = 2 * k + (c + d)
            if isinstance(number, int) and not 0 <= number < groups:
                return None
            return number, (c + d) % 2, k + (c + d) // 2
        return at

    assert groups % 2 == 1 and groups > 9
    for i in range(first, 2):
        step(of(0, i))
    with eng.Fori(0, (groups - 7) // 2) as k:
        step(of(k, 2))
        step(of(k, 3))
    for i in range(groups - 5, last + 1):
        step(of(0, i))


def stage(work, grp, *more):
    if grp is not None:
        work(grp, *more)


def in_turn(eng, groups, step):
    step((0, 0, 0))
    step((1, 1, 0))
    with eng.Fori(1, (groups - 1) // 2) as k:
        step((2 * k, 0, k))
        step((2 * k + 1, 1, k))
    step((groups - 1, 0, (groups - 1) // 2))


def gnn_kernel(nc, x, src, dst, ea, w, w_r, att_w, loop_w, fc1_w, w1, b1, w2, b2, out):
    N = x.shape[0]
    E = src.shape[0]
    TILES = -(-E // P)
    HALF = TILES // 2
    GROUPS = TILES // ET
    EG = ET * P
    NG = NT * P
    REST = E - (TILES - 1) * P
    assert TILES == 2 * HALF == ET * GROUPS and GROUPS % 2 == 1 and HALF <= P and 0 < REST < P
    assert (GROUPS - 1) * NG < N <= GROUPS * NG
    LAST_NODE = N - NG
    SLOT_USES = [GROUPS // 2 + 1, GROUPS // 2]

    ctx = ExitStack()
    with ctx:
        def sb(name, shape, dt=F32):
            return ctx.enter_context(nc.sbuf_tensor(name, shape, dt))

        def sem(name):
            return ctx.enter_context(nc.semaphore(name))

        def sem2(name):
            return [sem(f"{name}{b}") for b in range(2)]

        mg_dram = nc.dram_tensor("mg_scratch", [GROUPS, P, 2 * ET * DX], F32, kind="Internal").ap()
        filt_dram = nc.dram_tensor("filter_scratch", [GROUPS, P, EG], F32, kind="Internal").ap()

        ident = sb("ident", [P, P])
        wload = sb("wload", [P, 6, D])
        att = sb("att", [P, 3])
        loop_ext = sb("loop_ext", [P, DX])
        src_w = sb("src_w", [P, DX])
        rel_w = sb("rel_w", [P, DX])
        dst_w = sb("dst_w", [P, DX])
        fc1_t = sb("fc1_t", [P, D])
        w1_t = sb("w1_t", [P, D])
        w2_t = sb("w2_t", [P, D])
        b1_col = sb("b1_col", [P, 1])
        cap_b1 = sb("cap_b1", [P, 1])
        b2_col = sb("b2_col", [P, 1])
        b2_fold = sb("b2_fold", [P, 1])
        cap_b2 = sb("cap_b2", [P, 1])
        minus_log2 = sb("minus_log2", [P, P])

        xdst = sb("xdst", [P, TILES * D])
        score = sb("score", [P, TILES])
        cols = sb("cols", [P, TILES, 3])
        gidx = sb("gidx", [P, GROUPS, 2 * ET], I32)
        sidx = sb("sidx", [P, TILES], I32)

        src_i = sb("src_i", [HALF, 2, P], I32)
        dst_i = sb("dst_i", [HALF, 2, P], I32)
        nxt_i = sb("nxt_i", [HALF, 2, P], I32)
        dst_f = sb("dst_f", [HALF, 2, P])
        row_a = sb("row_a", [HALF, 2, P])
        row_b = sb("row_b", [HALF, 2, P])
        edge_cols = sb("edge_cols", [P, TILES])

        xn = sb("xn", [P, 2, NT, D])
        xs = sb("xs", [P, 2, 2 * ET, D])
        eab = sb("eab", [P, 2, ET, D])
        normed = sb("normed", [P, 2, LT, D])
        hT = sb("hT", [P, 5, EG])
        x1b = sb("x1b", [P, 2, NT, D])
        mg = sb("mg", [P, 2, 2 * ET, DX])
        filt = sb("filt", [P, 2, EG])
        soft = sb("soft", [P, 3, EG])
        stats = sb("stats", [P, 2, LT, 6])
        msum = sb("msum", [P, 2, LT])
        mdif = sb("mdif", [P, 2, LT])
        var4 = sb("var4", [P, 2, LT])
        ln_v = sb("ln_v", [P, 2, LT])
        guess = sb("guess", [P, 2, LT])
        newt = sb("newt", [P, 2, LT])
        rstd = sb("rstd", [P, 2, LT])
        nmr = sb("nmr", [P, 2, LT])
        gix = sb("gix", [P, 2, 2 * ET], I32)
        six = sb("six", [P, 2, ET], I32)
        drow = sb("drow", [P, 2, EG], I32)
        colb = sb("colb", [P, 2, ET, 3])
        same = xn[:, :, 0:ET, :]
        carry = xn[:, :, ET:2 * ET, :]
        agg = sb("agg", [P, 2, ET, DX])
        den = sb("den", [P, 2, ET])
        rden = sb("rden", [P, 2, ET])
        zsum = sb("zsum", [P, 2, ET])
        fresh = normed[0:HALF, 0, 0:2, :]
        fresh_back = normed[0:HALF, 0, 2:4, :]
        fwd = normed[0:HALF, 0, 4:6, :]
        bwd = normed[0:HALF, 0, 6:8, :]
        spread = normed[0:HALF, 0, 8:12, :].rearrange("p (q h) d -> p q h d", q=2)
        zkeep = normed[0:HALF, 0, 12:14, :]
        eps_col = sb("eps_col", [P, 1])
        cap_col = sb("cap_col", [P, 1])
        zmax = sb("zmax", [HALF, 2, 2])
        best = sb("best", [HALF, 1])
        tables = hT[0:HALF, 0:2, 0:2 * TILES]
        pick = hT[0:HALF, 2, 0:2 * TILES]

        bank = [ctx.enter_context(nc.psum_tensor(f"bank{i}", [P, 512], F32)) for i in range(8)]
        TB, PB, NB, WB = bank[0:2], bank[2:4], bank[4:6], bank[6:8]

        s_zero = sem("zeroed")
        s_ident = sem("ident_made")
        s_w = sem("weights_loaded")
        s_rows = sem("edge_rows_loaded")
        s_pads = sem("edge_rows_padded")
        s_pe0 = sem("setup_pe_done")
        s_dv0 = sem("setup_dve_done")
        s_idx = sem("indices_ready")
        s_wready = sem("weights_ready")
        s_lw = sem("setup_copies")

        x_in = sem2("nodes_loaded")
        ea_in = sem2("edge_attr_loaded")
        got_src = sem2("src_rows_gathered")
        got_dst = sem2("dst_rows_gathered")
        x_copied = sem2("nodes_copied")
        gix_set = sem("gather_index_set")
        kept = sem2("xdst_kept")
        s_stat = sem("stats_done")
        s_mom = sem("moment_steps")
        s_guess = sem("rstd_guessed")
        s_lnv = sem("ln_var_done")
        s_newt = sem("newton_steps")
        s_nd = sem("normed_by_dve")
        s_na = sem("normed_by_act")
        s_tp = sem("transposed")
        s_te = sem("transposes_evicted")
        s_mg = sem("mg_products")
        s_mge = sem("mg_evicted")
        s_w1 = sem("filter1_product")
        s_w2 = sem("filter2_product")
        s_p1 = sem("filter1_act_steps")
        s_p2 = sem("filter2_act_steps")
        s_sp1 = sem("filter1_done")
        s_sp2 = sem("filter2_done")
        s_nh = sem("node_products")
        s_x1 = sem("nodes_combined")
        s_z = sem("score_steps")
        x1_out = sem2("nodes_stored")
        mg_out = sem2("mg_stored")
        filt_out = sem2("filter_stored")

        s_sm_pe = sem("softmax_pe")
        s_sm_dve = sem("softmax_dve")
        s_sm_act = sem("softmax_act")
        s_cols = sem("softmax_done")

        mg_in = sem2("mg_loaded")
        dr_in = sem2("dst_rows_loaded")
        s_cb = sem("columns_copied")
        s_sel = sem("selections_built")
        s_ag = sem("sums_product")
        s_age = sem("sums_evicted")
        s_den = sem("weights_inverted")
        s_at = sem("attended")
        s_xo = sem("x1_rows_done")
        six_set = sem("scatter_index_set")
        scattered = sem2("x1_scattered")
        kept1 = sem2("x1_kept")

        gathered1 = sem2("x1_gathered")
        gix_set1 = sem("gather_index_set_1")
        filt_in = sem2("filter_loaded")
        dr_in1 = sem2("dst_rows_loaded_1")
        s_stat1 = sem("stats_done_1")
        s_mom1 = sem("moment_steps_1")
        s_lnv1 = sem("ln_var_done_1")
        s_guess1 = sem("rstd_guessed_1")
        s_newt1 = sem("newton_steps_1")
        s_n1 = sem("normed_1")
        s_tp1 = sem("transposed_1")
        s_te1 = sem("transposes_evicted_1")
        s_f1 = sem("fc1_product")
        s_msg = sem("messages_done")
        s_tm = sem("messages_transposed")
        s_me = sem("messages_evicted")
        s_cb1 = sem("columns_copied_1")
        s_sel1 = sem("selections_built_1")
        s_ag1 = sem("sums_product_1")
        s_age1 = sem("sums_evicted_1")
        s_add1 = sem("sums_added_1")
        s_buf = sem("rows_buffered")
        six_set1 = sem("scatter_index_set_1")
        put = sem2("out_scattered")

        dst_as_row = dst.rearrange("(a n) -> a n", a=1)

        def edge_base(g):
            return g * EG

        block = ctx.enter_context(nc.Block())

        @block.sync
        def _(sp):
            for n, a in enumerate((w, w_r, loop_w, fc1_w, w1, w2)):
                sp.dma_start(wload[:, n, :], a).then_inc(s_w, 16)
            sp.dma_start(att[:, :], att_w.rearrange("(t p) -> p t", p=P),
                         allow_slow_non_contiguous=True).then_inc(s_w, 16)
            sp.dma_start(b1_col[:, :], b1.rearrange("(p a) -> p a", a=1)).then_inc(s_w, 16)
            sp.dma_start(b2_col[:, :], b2.rearrange("(p a) -> p a", a=1)).then_inc(s_w, 16)
            sp.wait_ge(s_pads, 3)
            h1 = HALF * P
            full = (TILES - 1) * P
            for tile, a, off, rest in ((src_i, src, 0, REST), (dst_i, dst, 0, REST), (nxt_i, dst, 1, REST - 1)):
                sp.dma_start(tile[:, 0, :], a[off:off + h1].rearrange("(t p) -> t p", p=P)).then_inc(s_rows, 16)
                sp.dma_start(tile[0:HALF - 1, 1, :],
                             a[off + h1:off + full].rearrange("(t p) -> t p", p=P)).then_inc(s_rows, 16)
                sp.dma_start(tile[HALF - 1:HALF, 1, 0:rest],
                             a[off + full:E].rearrange("(a n) -> a n", a=1)).then_inc(s_rows, 16)

            def load_nodes(grp):
                g, b, n = grp
                wait_apart(sp, x_copied[b], 16 * n)
                wait_apart(sp, s_na, NORM_ACT * (g - 1))
                wait_apart(sp, s_nd, NORM_DVE * (g - 1))
                start = LAST_NODE if isinstance(g, int) and g == GROUPS - 1 else g * NG
                sp.dma_start(xn[:, b, :, :].rearrange("p t d -> p (t d)"),
                             x[bass.ds(start, NG), :].rearrange("(p t) d -> p (t d)", p=P)).then_inc(x_in[b], 16)

            def load_edges(grp):
                g, b, n = grp
                final = isinstance(g, int) and g == GROUPS - 1
                if isinstance(g, int) and g == 0:
                    sp.wait_ge(s_zero, 1)
                wait_apart(sp, s_tp, 5 * g - 7)
                tiles = ET - 1 if final else ET
                sp.dma_start(eab[:, b, 0:tiles, :], ea[bass.ds(edge_base(g), tiles * P), :]
                             .rearrange("(t p) d -> p t d", p=P)).then_inc(ea_in[b], 16)
                if final:
                    sp.dma_start(eab[0:REST, b, ET - 1, :], ea[E - REST:E, :]).then_inc(ea_in[b], 16)

            def keep_dst(grp):
                g, b, n = grp
                wait_apart(sp, got_dst[b], 16 * ET * (n + 1))
                sp.dma_start(xdst[:, bass.ds(g * EG, EG)],
                             xs[:, b, ET:2 * ET, :].rearrange("p t d -> p (t d)")).then_inc(kept[b], 16)

            def copy_nodes(grp):
                g, b, n = grp
                wait_apart(sp, x_in[b], 16 * (n + 1))
                wait_apart(sp, x1_out[b], 16 * n)
                sp.dma_start(x1b[:, b, :, :], xn[:, b, :, :]).then_inc(x_copied[b], 16)

            def store_nodes(grp):
                g, b, n = grp
                wait_apart(sp, s_x1, 2 * (g + 1))
                start = g * NG
                if isinstance(g, int) and g == GROUPS - 1:
                    start = LAST_NODE
                    for c in range(2):
                        sp.wait_ge(x1_out[c], 16 * (GROUPS // 2))
                sp.dma_start(out[bass.ds(start, NG), :].rearrange("(p t) d -> p (t d)", p=P),
                             x1b[:, b, :, :].rearrange("p t d -> p (t d)")).then_inc(x1_out[b], 16)

            def store_mg(grp):
                g, b, n = grp
                wait_apart(sp, s_z, 3 * (g + 1))
                sp.dma_start(mg_dram[g], mg[:, b, :, :].rearrange("p t d -> p (t d)")).then_inc(mg_out[b], 16)

            def store_filter(grp):
                g, b, n = grp
                wait_apart(sp, s_sp2, g + 1)
                sp.dma_start(filt_dram[g], filt[:, b, :]).then_inc(filt_out[b], 16)

            def node_and_edge(at):
                stage(store_nodes, at(-1))
                stage(keep_dst, at(1))
                stage(store_mg, at(-1))
                stage(copy_nodes, at(1))
                stage(load_edges, at(2))
                stage(store_filter, at(-1))
                stage(load_nodes, at(3))

            staged(sp, GROUPS, -3, GROUPS, node_and_edge)

            for b in range(2):
                sp.wait_ge(mg_out[b], 16 * SLOT_USES[b])

            def dst_rows(grp, done, target):
                g, b, n = grp
                final = isinstance(g, int) and g == GROUPS - 1
                count = E - (GROUPS - 1) * EG if final else EG
                wait_apart(sp, done, 2 * ET * (g - 1))
                sp.dma_start(drow[:, b, 0:count],
                             dst_as_row[:, bass.ds(edge_base(g), count)].partition_broadcast(P)).then_inc(target[b], 16)

            def load_mg(grp):
                g, b, n = grp
                wait_apart(sp, s_xo, g - 1)
                sp.dma_start(mg[:, b, :, :].rearrange("p t d -> p (t d)"), mg_dram[g]).then_inc(mg_in[b], 16)

            def keep_x1(grp):
                g, b, n = grp
                wait_apart(sp, s_xo, g + 1)
                sp.dma_start(xdst[:, bass.ds(g * EG, EG)],
                             x1b[:, b, 0:ET, :].rearrange("p t d -> p (t d)")).then_inc(kept1[b], 16)

            def attend(at):
                stage(dst_rows, at(2), s_sel, dr_in)
                stage(keep_x1, at(0))
                stage(load_mg, at(2))

            staged(sp, GROUPS, -2, GROUPS - 1, attend)

            for b in range(2):
                sp.wait_ge(filt_out[b], 16 * SLOT_USES[b])
            sp.wait_ge(s_sel, 2 * ET * GROUPS)

            def load_filter(grp):
                g, b, n = grp
                wait_apart(sp, s_msg, g - 1)
                sp.dma_start(filt[:, b, :], filt_dram[g]).then_inc(filt_in[b], 16)

            def convolve(at):
                stage(dst_rows, at(2), s_sel1, dr_in1)
                stage(load_filter, at(2))

            staged(sp, GROUPS, -2, GROUPS - 3, convolve)
            for b in range(2):
                sp.wait_ge(x1_out[b], 16 * SLOT_USES[b])
                sp.wait_ge(put[b], 16 * ET * SLOT_USES[b])

        @block.gpsimd
        def _(pool):
            nc.gpsimd.memset(src_i[:, :, :], 0).then_inc(s_pads, 1)
            nc.gpsimd.memset(dst_i[:, :, :], int(PAD_DST)).then_inc(s_pads, 1)
            nc.gpsimd.memset(nxt_i[:, :, :], int(PAD_DST)).then_inc(s_pads, 1)
            nc.gpsimd.memset(ident[:, :], 0.0).then_inc(s_ident, 1)
            pool.wait_ge(s_ident, 1)
            nc.gpsimd.affine_select(out=ident[:, :], in_=ident[:, :], compare_op=ALU.not_equal, fill=1.0,
                                    base=0, pattern=[[-1, P]], channel_multiplier=1).then_inc(s_ident, 1)
            nc.gpsimd.memset(minus_log2[:, :], -LOG2).then_inc(s_ident, 1)
            nc.gpsimd.memset(eab[:, :, :, :], 0.0).then_inc(s_zero, 1)
            nc.gpsimd.memset(agg[:, :, :, :], 0.0).then_inc(s_zero, 1)
            nc.gpsimd.memset(drow[:, :, :], int(PAD_DST)).then_inc(s_zero, 1)

            pool.wait_ge(s_idx, 1)

            def gather(grp):
                g, b, n = grp
                wait(pool, got_src[b], 16 * ET * n)
                wait_apart(pool, got_dst[b], 16 * ET * n)
                nc.gpsimd.tensor_copy(gix[:, b, :], gidx[:, bass.ds(g, 1), :]
                                      .rearrange("p a t -> p (a t)")).then_inc(gix_set, 1)
                wait_apart(pool, gix_set, g + 1)
                for t in range(2 * ET):
                    if t % ET == 0:
                        wait_apart(pool, s_nd, NORM_DVE * g - 2 * NORM_DVE + t + ET)
                    if t == ET:
                        wait_apart(pool, kept[b], 16 * n)
                    pool.indirect_dma_start(xs[:, b, t, :], None, x, bass.IndirectOffsetOnAxis(gix[:, b, t:t + 1], 0)
                                            ).then_inc(got_src[b] if t < ET else got_dst[b], 16)

            in_turn(pool, GROUPS, gather)

            for b in range(2):
                pool.wait_ge(x1_out[b], 16 * SLOT_USES[b])

            def scatter(grp, done, index_set, data):
                g, b, n = grp
                if not (isinstance(g, int) and g < 2):
                    wait_apart(pool, done[b], 16 * ET * n)
                nc.gpsimd.tensor_copy(six[:, b, :], sidx[:, bass.ds(g * ET, ET)]).then_inc(index_set, 1)
                pool.wait_ge(index_set, g + 1)
                wait_apart(pool, data, g + 1)
                for t in range(ET):
                    pool.indirect_dma_start(out, bass.IndirectOffsetOnAxis(six[:, b, t:t + 1], 0), x1b[:, b, t, :],
                                            None, bounds_check=N - 1, oob_is_err=False).then_inc(done[b], 16)

            in_turn(pool, GROUPS, lambda grp: scatter(grp, scattered, six_set, s_xo))

            for b in range(2):
                pool.wait_ge(scattered[b], 16 * ET * SLOT_USES[b])

            def gather_again(grp):
                g, b, n = grp
                if not (isinstance(g, int) and g < 2):
                    pool.wait_ge(gathered1[b], 16 * ET * n)
                    wait_apart(pool, s_n1, ET * (g - 1))
                nc.gpsimd.tensor_copy(gix[:, b, 0:ET], gidx[:, bass.ds(g, 1), 0:ET]
                                      .rearrange("p a t -> p (a t)")).then_inc(gix_set1, 1)
                wait_apart(pool, gix_set1, g + 1)
                for t in range(ET):
                    pool.indirect_dma_start(xs[:, b, t, :], None, out,
                                            bass.IndirectOffsetOnAxis(gix[:, b, t:t + 1], 0)).then_inc(gathered1[b], 16)

            in_turn(pool, GROUPS, gather_again)

            for b in range(2):
                pool.wait_ge(gathered1[b], 16 * ET * SLOT_USES[b])
            in_turn(pool, GROUPS, lambda grp: scatter(grp, put, six_set1, s_buf))
            for b in range(2):
                pool.wait_ge(put[b], 16 * ET * SLOT_USES[b])

        @block.tensor
        def _(pe):
            pe.wait_ge(s_ident, 3)
            pe.wait_ge(s_w, 16 * 9)
            for n, i in enumerate((0, 1, 3, 4)):
                last = pe.transpose(bank[0][:, n * D:(n + 1) * D], wload[:, i, :], ident[:, :])
            last.then_inc(s_pe0, 1)
            pe.transpose(bank[1][:, 0:D], wload[:, 5, :], ident[:, :]).then_inc(s_pe0, 1)
            pe.wait_ge(s_dv0, 1)
            pe.matmul(bank[2][:, 0:DX], wload[:, 0, :], loop_ext[:, :], start=True, stop=True)
            pe.matmul(bank[2][:, 256:257], wload[:, 0, :], att[:, 0:1], start=True, stop=True)
            pe.matmul(bank[2][:, 260:261], wload[:, 1, :], att[:, 2:3], start=True, stop=True).then_inc(s_pe0, 1)
            pe.wait_ge(s_dv0, 3)
            pe.matmul(bank[3][:, 0:1], w2_t[:, :], minus_log2[:, 0:1], start=True, stop=True).then_inc(s_pe0, 1)
            for q in range(4):
                pe.wait_ge(s_dv0, 6 + 2 * q)
                for h in range(2):
                    last = pe.transpose(bank[4][:, h * HALF:(h + 1) * HALF],
                                        (row_a if q < 3 else dst_f)[:, h, :], ident[0:HALF, 0:HALF])
                last.then_inc(s_pe0, 1)

            pe.wait_ge(s_wready, 1)

            def transposes(grp, i, source, psum):
                g, b, n = grp
                q = 5 * g + i
                wait(pe, s_te, q - 1)
                for t in range(ET):
                    last = pe.transpose(psum[:, t * P:(t + 1) * P], source(t), ident[:, :])
                last.then_inc(s_tp, 1)

            def pair(grp, lo, r):
                g, b, n = grp
                wait(pe, s_mge, 4 * g + r - 1)
                psum = PB[r % 2]
                for t in range(lo, lo + 2):
                    o = psum[:, (t - lo) * DX:(t - lo + 1) * DX]
                    tile = slice(t * P, (t + 1) * P)
                    if r % 2 == 0:
                        last = pe.matmul(o, hT[:, 1, tile], dst_w[:, :], start=True, stop=True)
                    else:
                        pe.matmul(o, hT[:, 0, tile], src_w[:, :], start=True, stop=False)
                        last = pe.matmul(o, hT[:, 2, tile], rel_w[:, :], start=False, stop=True)
                last.then_inc(s_mg, 1)

            def node_half(grp, half):
                g, b, n = grp
                pe.wait_ge(s_te, 5 * g + 4 + half)
                wait(pe, s_x1, 2 * g - 1 + half)
                for t in range(4):
                    last = pe.matmul(NB[half][:, t * D:(t + 1) * D], hT[:, 3 + half, t * P:(t + 1) * P],
                                     src_w[:, 0:D], start=True, stop=True)
                last.then_inc(s_nh, 1)

            def second_filter(grp):
                g, b, n = grp
                pe.wait_ge(s_sp1, g + 1)
                wait(pe, s_sp2, g)
                pe.matmul(WB[1][:, :], w2_t[:, :], soft[:, 2, :], start=True, stop=True).then_inc(s_w2, 1)

            def node_and_edge(at):
                grp = at(0)
                if grp is None:
                    stage(second_filter, at(-1))
                    return
                g, b, n = grp
                pe.wait_ge(s_nd, NORM_DVE * g + 2 * ET)
                transposes(grp, 0, lambda t: normed[:, b, NT + t, :], TB[b])
                transposes(grp, 1, lambda t: normed[:, b, NT + ET + t, :], TB[1 - b])
                stage(second_filter, at(-1))
                pe.wait_ge(ea_in[b], 16 * (n + 1) + (16 if isinstance(g, int) and g == GROUPS - 1 else 0))
                transposes(grp, 2, lambda t: eab[:, b, t, :], TB[b])
                pe.wait_ge(s_nd, NORM_DVE * (g + 1))
                pe.wait_ge(s_na, NORM_ACT * (g + 1))
                transposes(grp, 3, lambda t: normed[:, b, t, :], TB[1 - b])
                pe.wait_ge(s_te, 5 * g + 2)
                pair(grp, 0, 0)
                pe.wait_ge(s_te, 5 * g + 3)
                wait(pe, s_sp1, g)
                pe.matmul(WB[0][:, :], w1_t[:, :], hT[:, 2, :], start=True, stop=True).then_inc(s_w1, 1)
                pair(grp, 0, 1)
                transposes(grp, 4, lambda t: normed[:, b, 4 + t, :], TB[b])
                pair(grp, 2, 2)
                node_half(grp, 0)
                pair(grp, 2, 3)
                node_half(grp, 1)

            staged(pe, GROUPS, 0, GROUPS, node_and_edge)

            pe.wait_ge(s_z, 3 * GROUPS)
            pe.wait_ge(s_te, 5 * GROUPS)
            for h in range(2):
                last = pe.transpose(bank[0][0:HALF, h * P:(h + 1) * P], score[:, h * HALF:(h + 1) * HALF], ident[:, :])
            last.then_inc(s_sm_pe, 1)
            for q in range(4):
                pe.wait_ge(s_sm_dve, SM_BCAST + q)
                for h in range(2):
                    last = pe.transpose(bank[1 + q // 2][:, (q % 2) * TILES + h * HALF:(q % 2) * TILES + (h + 1) * HALF],
                                        spread[:, q % 2, h, :], ident[0:HALF, 0:HALF])
                last.then_inc(s_sm_pe, 1)
            pe.wait_ge(s_sm_act, 1)
            for h in range(2):
                last = pe.transpose(bank[3][:, h * HALF:(h + 1) * HALF], row_b[:, h, :], ident[0:HALF, 0:HALF])
            last.then_inc(s_sm_pe, 1)

            def own(grp, j, rows, width, selected, evicted):
                g, b, n = grp
                pe.wait_ge(selected, 2 * ET * g + 2 * j + 2)
                wait(pe, evicted, ET * g + j - ET + 1)
                pe.matmul(bank[j][:, 0:width], same[:, b, j, :], rows, start=True, stop=False)

            def carried(grp, j, width, evicted, made):
                g, b, n = grp
                wait(pe, evicted, ET * g + j)
                before = agg[:, b, j - 1, 0:width] if j else agg[:, 1 - b, ET - 1, 0:width]
                pe.matmul(bank[j][:, 0:width], carry[:, b, j, :], before, start=False, stop=True).then_inc(made, 1)

            def attend(grp):
                g, b, n = grp
                pe.wait_ge(mg_in[b], 16 * (n + 1))
                own(grp, 0, mg[:, b, 0, :], DX, s_sel, s_age)
                for j in range(ET):
                    if j + 1 < ET:
                        own(grp, j + 1, mg[:, b, j + 1, :], DX, s_sel, s_age)
                    carried(grp, j, DX, s_age, s_ag)

            pe.wait_ge(s_cols, 1)
            pe.wait_ge(s_zero, 3)
            in_turn(pe, GROUPS, attend)

            pe.wait_ge(s_den, 2 * GROUPS)

            def turn_x1(grp):
                g, b, n = grp
                pe.wait_ge(s_n1, ET * (g + 1))
                wait(pe, s_te1, g)
                for t in range(ET):
                    last = pe.transpose(bank[4][:, t * P:(t + 1) * P], normed[:, b, t, :], ident[:, :])
                last.then_inc(s_tp1, 1)

            def project(grp):
                g, b, n = grp
                pe.wait_ge(s_te1, g + 1)
                wait(pe, s_msg, g)
                pe.matmul(bank[5][:, :], fc1_t[:, :], hT[:, 0, :], start=True, stop=True).then_inc(s_f1, 1)

            def turn_messages(grp):
                g, b, n = grp
                pe.wait_ge(s_msg, g + 1)
                wait(pe, s_me, g)
                for t in range(ET):
                    last = pe.transpose(bank[6][:, t * P:(t + 1) * P], hT[:, 1, t * P:(t + 1) * P], ident[:, :])
                last.then_inc(s_tm, 1)

            def sum_tile(grp, j, part):
                g, b, n = grp
                if part == 0:
                    if j == 0:
                        pe.wait_ge(s_me, g + 1)
                    own(grp, j, x1b[:, b, ET + j, :], D, s_sel1, s_age1)
                else:
                    carried(grp, j, D, s_age1, s_ag1)

            def convolve(at):
                stage(sum_tile, at(-1), 0, 0)
                stage(sum_tile, at(-1), 0, 1)
                stage(turn_x1, at(0))
                stage(sum_tile, at(-1), 1, 0)
                stage(sum_tile, at(-1), 1, 1)
                stage(sum_tile, at(-1), 2, 0)
                stage(project, at(0))
                stage(sum_tile, at(-1), 2, 1)
                stage(sum_tile, at(-1), 3, 0)
                stage(sum_tile, at(-1), 3, 1)
                stage(turn_messages, at(0))

            staged(pe, GROUPS, 0, GROUPS, convolve)

        @block.scalar
        def _(act):
            act.preload_act_table_set("natural_log_exp_and_others")

            def guess_rstd(grp, moments, ln_done, guessed, lt):
                g, b, n = grp
                act.wait_ge(moments, 5 * (g + 1))
                act.activation(ln_v[:, b, 0:lt], var4[:, b, 0:lt], ACT.Ln, scale=0.25, bias=eps_col[:, 0:1]).then_inc(ln_done, 1)
                act.wait_ge(ln_done, g + 1)
                act.activation(guess[:, b, 0:lt], ln_v[:, b, 0:lt], ACT.Exp, scale=-0.5).then_inc(guessed, 1)

            def normalize(grp):
                g, b, n = grp
                act.wait_ge(s_newt, 5 * (g + 1))
                wait(act, s_tp, 5 * (g - 1))
                for t in range(NORM_ACT):
                    act.activation(normed[:, b, t, :], xn[:, b, t, :], ACT.Identity,
                                   bias=nmr[:, b, t:t + 1], scale=rstd[:, b, t:t + 1]).then_inc(s_na, 1)

            def evict(grp, i):
                g, b, n = grp
                act.wait_ge(s_tp, 5 * g + i + 1)
                if i < 3:
                    wait(act, s_mg, 4 * g)
                else:
                    wait(act, s_nh, 2 * g - 4 + i)
                act.activation(hT[:, i, :], TB[(b + i) % 2][:, :], ACT.Copy if i == 2 else ACT.Relu).then_inc(s_te, 1)

            def evict_pair(grp, r):
                g, b, n = grp
                act.wait_ge(s_mg, 4 * g + r + 1)
                if r == 0:
                    wait(act, mg_out[b], 16 * n)
                lo = (r // 2) * 2 + (ET if r % 2 == 0 else 0)
                act.copy(mg[:, b, lo:lo + 2, :].rearrange("p t d -> p (t d)"), PB[r % 2][:, 0:2 * DX]).then_inc(s_mge, 1)

            def softplus_step(grp, layer, k):
                g, b, n = grp
                buf, steps, used = soft[:, layer, :], (s_p1, s_p2)[layer], (s_sp1, s_sp2)[layer]
                if k == 0:
                    act.wait_ge((s_w1, s_w2)[layer], g + 1)
                    wait(act, used, g)
                    act.activation(buf, WB[layer][:, :], ACT.Relu, scale=-1.0,
                                   bias=(cap_b1, cap_b2)[layer][:, 0:1]).then_inc(steps, 1)
                    return
                act.wait_ge(steps, 3 * g + k)
                if k == 1:
                    act.activation(buf, buf, ACT.Exp, scale=-1.0, bias=cap_col[:, 0:1]).then_inc(steps, 1)
                else:
                    act.activation(buf, buf, ACT.Ln, bias=1.0).then_inc(steps, 1)

            def node_and_edge(at):
                stage(guess_rstd, at(1), s_mom, s_lnv, s_guess, LT)
                stage(evict, at(0), 0)
                stage(evict, at(0), 1)
                stage(softplus_step, at(-1), 1, 0)
                stage(evict, at(0), 2)
                stage(softplus_step, at(-1), 1, 1)
                stage(evict, at(0), 3)
                stage(softplus_step, at(-1), 1, 2)
                stage(evict_pair, at(0), 0)
                stage(softplus_step, at(0), 0, 0)
                stage(evict_pair, at(0), 1)
                stage(softplus_step, at(0), 0, 1)
                stage(evict, at(0), 4)
                stage(softplus_step, at(0), 0, 2)
                stage(evict_pair, at(0), 2)
                stage(evict_pair, at(0), 3)
                stage(normalize, at(1))

            act.wait_ge(s_wready, 1)
            staged(act, GROUPS, -1, GROUPS, node_and_edge)

            act.wait_ge(s_sm_dve, SM_SHIFTED)
            act.activation(row_b[:, :, :], row_a[:, :, :], ACT.Exp).then_inc(s_sm_act, 1)

            def evict_sum(grp, j, width, ready, evicted, used, per):
                g, b, n = grp
                act.wait_ge(ready, ET * g + j + 1)
                if j == 0:
                    wait(act, used, per * (g - 1))
                act.copy(agg[:, b, j, 0:width], bank[j][:, 0:width]).then_inc(evicted, 1)

            def evict_sums(grp):
                for j in range(ET):
                    evict_sum(grp, j, DX, s_ag, s_age, s_at, ET)

            act.wait_ge(s_zero, 3)
            in_turn(act, GROUPS, evict_sums)

            def normalize_x1(grp):
                g, b, n = grp
                act.wait_ge(s_newt1, 5 * (g + 1))
                wait(act, s_tp1, g - 1)
                for t in range(ET):
                    act.activation(normed[:, b, t, :], xs[:, b, t, :], ACT.Identity,
                                   bias=nmr[:, b, t:t + 1], scale=rstd[:, b, t:t + 1]).then_inc(s_n1, 1)

            def evict_x1(grp):
                g, b, n = grp
                act.wait_ge(s_tp1, g + 1)
                wait(act, s_f1, g)
                act.activation(hT[:, 0, :], bank[4][:, :], ACT.Relu).then_inc(s_te1, 1)

            def evict_messages(grp):
                g, b, n = grp
                act.wait_ge(s_tm, g + 1)
                wait(act, s_ag1, ET * (g - 1))
                act.copy(x1b[:, b, ET:2 * ET, :].rearrange("p t d -> p (t d)"), bank[6][:, :]).then_inc(s_me, 1)

            def convolve(at):
                def sums(j):
                    stage(evict_sum, at(-1), j, D, s_ag1, s_age1, s_add1, 1)

                stage(guess_rstd, at(1), s_mom1, s_lnv1, s_guess1, ET)
                sums(0)
                stage(evict_x1, at(0))
                sums(1)
                sums(2)
                sums(3)
                stage(normalize_x1, at(1))
                stage(evict_messages, at(0))

            act.wait_ge(s_at, ET * GROUPS)
            staged(act, GROUPS, -1, GROUPS, convolve)

            def buffer_rows(grp):
                g, b, n = grp
                if not (isinstance(g, int) and g < 2):
                    act.wait_ge(put[b], 16 * ET * n)
                act.copy(x1b[:, b, 0:ET, :].rearrange("p t d -> p (t d)"),
                         xdst[:, bass.ds(g * EG, EG)]).then_inc(s_buf, 1)

            act.wait_ge(s_add1, GROUPS)
            act.wait_ge(scattered[0], 16 * ET * SLOT_USES[0])
            act.wait_ge(scattered[1], 16 * ET * SLOT_USES[1])
            in_turn(act, GROUPS, buffer_rows)

        @block.vector
        def _(dve):
            v = nc.vector
            done = [0]

            def setup(ins):
                done[0] += 1
                ins.then_inc(s_dv0, 1)
                dve.wait_ge(s_dv0, done[0])

            v.memset(eps_col[:, :], EPS).then_inc(s_lw, 1)
            v.memset(cap_col[:, :], CAP).then_inc(s_lw, 1)
            dve.wait_ge(s_w, 16 * 9)
            v.tensor_copy(loop_ext[:, 0:D], wload[:, 2, :]).then_inc(s_lw, 1)
            setup(v.tensor_copy(loop_ext[:, D:DX], att[:, 1:2]))
            setup(v.tensor_scalar(cap_b1[:, :], b1_col[:, :], -1.0, CAP, ALU.mult, ALU.add))
            dve.wait_ge(s_pe0, 2)
            setup(v.tensor_copy(w2_t[:, :], bank[1][:, 0:D]))
            for n, dest in enumerate((src_w, rel_w, fc1_t, w1_t)):
                v.tensor_copy(dest[:, 0:D], bank[0][:, n * D:(n + 1) * D]).then_inc(s_lw, 1)
            dve.wait_ge(s_pe0, 3)
            v.tensor_copy(dst_w[:, :], bank[2][:, 0:DX]).then_inc(s_lw, 1)
            v.tensor_copy(src_w[:, D:DX], bank[2][:, 256:257]).then_inc(s_lw, 1)
            v.tensor_copy(rel_w[:, D:DX], bank[2][:, 260:261]).then_inc(s_lw, 1)
            dve.wait_ge(s_pe0, 4)
            v.tensor_tensor(b2_fold[:, :], bank[3][:, 0:1], b2_col[:, :], ALU.add).then_inc(s_lw, 1)
            dve.wait_ge(s_lw, 11)
            v.tensor_scalar(cap_b2[:, :], b2_fold[:, :], -1.0, CAP, ALU.mult, ALU.add).then_inc(s_lw, 1)
            dve.wait_ge(s_rows, 16 * 9)
            setup(v.tensor_copy(dst_f[:, :, :], dst_i[:, :, :]))
            setup(v.tensor_copy(row_b[:, :, :], nxt_i[:, :, :]))
            setup(v.tensor_copy(row_a[:, :, :], src_i[:, :, :]))
            grouped = [bank[4][:, 0:TILES].rearrange("p (g t) -> p g t", t=ET)]
            dve.wait_ge(s_pe0, 5)
            setup(v.tensor_copy(gidx[:, :, 0:ET], grouped[0]))
            setup(v.tensor_scalar(row_a[:, :, :], dst_f[:, :, :], float(N - 1), None, ALU.min))
            dve.wait_ge(s_pe0, 6)
            setup(v.tensor_copy(gidx[:, :, ET:2 * ET], grouped[0]))
            v.tensor_tensor(row_b[:, :, :], dst_f[:, :, :], row_b[:, :, :], ALU.is_equal).then_inc(s_lw, 1)
            dve.wait_ge(s_lw, 13)
            setup(v.scalar_tensor_tensor(out=row_a[:, :, :], in0=row_b[:, :, :], scalar=SKIP, in1=dst_f[:, :, :],
                                         op0=ALU.mult, op1=ALU.add))
            dve.wait_ge(s_pe0, 7)
            setup(v.tensor_copy(sidx[:, :], bank[4][:, 0:TILES]))
            setup(v.memset(cols[:, 0:1, 2], -1.0))
            dve.wait_ge(s_pe0, 8)
            v.tensor_copy(edge_cols[:, :], bank[4][:, 0:TILES]).then_inc(s_lw, 1)
            dve.wait_ge(s_lw, 14)
            v.tensor_copy(cols[:, :, 0], edge_cols[:, :]).then_inc(s_lw, 1)
            v.tensor_scalar(cols[:, 1:TILES, 2], edge_cols[:, 0:TILES - 1], 1.0, ident[:, P - 1:P],
                            ALU.add, ALU.mult).then_inc(s_lw, 1)
            dve.wait_ge(s_lw, 16)
            v.tensor_scalar(cols[:, 1:TILES, 2], cols[:, 1:TILES, 2], -1.0, None, ALU.add).then_inc(s_lw, 1)
            dve.wait_ge(s_lw, 17)
            v.memset(den[:, :, :], 1.0).then_inc(s_idx, 1)
            dve.wait_ge(s_idx, 1)
            v.memset(rden[:, :, :], 1.0).then_inc(s_wready, 1)

            def moments(grp, stat, steps, lt, tile):
                g, b, n = grp
                for t in range(lt):
                    tile(t)
                dve.wait_ge(stat, lt * (g + 1))
                mean_e, mean_o = stats[:, b, 0:lt, 1], stats[:, b, 0:lt, 4]
                dif, var = mdif[:, b, 0:lt], var4[:, b, 0:lt]
                v.tensor_tensor(dif, mean_e, mean_o, ALU.subtract).then_inc(steps, 1)
                v.tensor_tensor(var, stats[:, b, 0:lt, 2], stats[:, b, 0:lt, 5], ALU.add).then_inc(steps, 1)
                v.tensor_tensor(msum[:, b, 0:lt], mean_e, mean_o, ALU.add).then_inc(steps, 1)
                dve.wait_ge(steps, 5 * g + 1)
                v.tensor_tensor(dif, dif, dif, ALU.mult).then_inc(steps, 1)
                dve.wait_ge(steps, 5 * g + 4)
                v.scalar_tensor_tensor(out=var, in0=var, scalar=4.0 / D, in1=dif,
                                       op0=ALU.mult, op1=ALU.add).then_inc(steps, 1)

            def newton(grp, guessed, steps, lt):
                g, b, n = grp
                y, u = guess[:, b, 0:lt], newt[:, b, 0:lt]
                dve.wait_ge(guessed, g + 1)
                v.tensor_tensor(u, y, y, ALU.mult).then_inc(steps, 1)
                dve.wait_ge(steps, 5 * g + 1)
                v.scalar_tensor_tensor(out=u, in0=var4[:, b, 0:lt], scalar=4 * EPS, in1=u,
                                       op0=ALU.add, op1=ALU.mult).then_inc(steps, 1)
                dve.wait_ge(steps, 5 * g + 2)
                v.tensor_scalar(u, u, -0.125, 1.5, ALU.mult, ALU.add).then_inc(steps, 1)
                dve.wait_ge(steps, 5 * g + 3)
                v.tensor_tensor(rstd[:, b, 0:lt], y, u, ALU.mult).then_inc(steps, 1)
                dve.wait_ge(steps, 5 * g + 4)
                v.scalar_tensor_tensor(out=nmr[:, b, 0:lt], in0=msum[:, b, 0:lt], scalar=-0.5,
                                       in1=rstd[:, b, 0:lt], op0=ALU.mult, op1=ALU.mult).then_inc(steps, 1)

            def take_moments(grp):
                g, b, n = grp
                dve.wait_ge(x_in[b], 16 * (n + 1))

                def tile(t):
                    if t == NT:
                        dve.wait_ge(got_src[b], 16 * ET * (n + 1))
                    if t == NT + ET:
                        dve.wait_ge(got_dst[b], 16 * ET * (n + 1))
                    v.bn_stats(stats[:, b, t, :], xn[:, b, t, :] if t < NT else xs[:, b, t - NT, :]).then_inc(s_stat, 1)

                moments(grp, s_stat, s_mom, LT, tile)

            def normalize(grp):
                g, b, n = grp
                newton(grp, s_guess, s_newt, LT)
                wait(dve, s_tp, 5 * (g - 1))
                dve.wait_ge(s_newt, 5 * (g + 1))
                for t in (*range(NT, LT), *range(NORM_ACT, NT)):
                    v.tensor_scalar(normed[:, b, t, :], xn[:, b, t, :] if t < NT else xs[:, b, t - NT, :],
                                    rstd[:, b, t:t + 1], nmr[:, b, t:t + 1], ALU.mult, ALU.add).then_inc(s_nd, 1)

            def first_filter(grp):
                g, b, n = grp
                dve.wait_ge(s_p1, 3 * (g + 1))
                wait(dve, s_w2, g)
                v.scalar_tensor_tensor(out=soft[:, 2, :], in0=WB[0][:, :], scalar=b1_col[:, 0:1], in1=soft[:, 0, :],
                                       op0=ALU.add, op1=ALU.max).then_inc(s_sp1, 1)

            def second_filter(grp):
                g, b, n = grp
                dve.wait_ge(s_p2, 3 * (g + 1))
                wait(dve, filt_out[b], 16 * n)
                v.scalar_tensor_tensor(out=filt[:, b, :], in0=WB[1][:, :], scalar=b2_fold[:, 0:1], in1=soft[:, 1, :],
                                       op0=ALU.add, op1=ALU.max).then_inc(s_sp2, 1)

            def combine_nodes(grp):
                g, b, n = grp
                dve.wait_ge(x_copied[b], 16 * (n + 1))
                for half in range(2):
                    dve.wait_ge(s_nh, 2 * g + half + 1)
                    rows = x1b[:, b, 4 * half:4 * half + 4, :].rearrange("p t d -> p (t d)")
                    v.scalar_tensor_tensor(out=rows, in0=NB[half][:, :], scalar=0.0, in1=rows,
                                           op0=ALU.max, op1=ALU.add).then_inc(s_x1, 1)

            def scores(grp):
                g, b, n = grp
                dve.wait_ge(s_mge, 4 * (g + 1))
                v.tensor_tensor(zsum[:, b, :], mg[:, b, 0:ET, D], mg[:, b, ET:2 * ET, D], ALU.add).then_inc(s_z, 1)
                dve.wait_ge(s_z, 3 * g + 1)
                v.scalar_tensor_tensor(out=score[:, bass.ds(g * ET, ET)], in0=zsum[:, b, :], scalar=0.01,
                                       in1=zsum[:, b, :], op0=ALU.mult, op1=ALU.max).then_inc(s_z, 1)
                v.memset(mg[:, b, 0:ET, D], 1.0).then_inc(s_z, 1)

            def node_and_edge(at):
                stage(combine_nodes, at(-1))
                stage(normalize, at(1))
                stage(scores, at(-1))
                stage(second_filter, at(-1))
                stage(take_moments, at(2))
                stage(first_filter, at(0))

            staged(dve, GROUPS, -2, GROUPS, node_and_edge)

            count = [0]

            def sm(ins):
                count[0] += 1
                ins.then_inc(s_sm_dve, 1)
                dve.wait_ge(s_sm_dve, count[0])

            flat = "p h e -> p (h e)"
            dve.wait_ge(s_sm_pe, 1)
            zr = row_a
            sm(v.tensor_copy(zr[:, :, :].rearrange(flat), bank[0][0:HALF, 0:2 * P]))
            sm(v.memset(fresh[:, :, :], -FAR))
            sm(v.tensor_tensor(fresh[:, :, 1:P], dst_f[:, :, 1:P], dst_f[:, :, 0:P - 1], ALU.not_equal))
            sm(v.tensor_scalar(fresh[:, :, 1:P], fresh[:, :, 1:P], -FAR, None, ALU.mult))
            sm(v.memset(fresh_back[:, :, :], -FAR))
            sm(v.tensor_copy(fresh_back[:, :, 0:P - 1], fresh[:, :, 1:P]))

            def run_max(forward, backward):
                a, z = fresh[:, :, :].rearrange(flat), zr[:, :, :].rearrange(flat)
                ab = fresh_back[:, :, :].rearrange(flat)
                sm(v.tensor_tensor_scan(forward[:, :, :].rearrange(flat), a, z, -FAR, ALU.add, ALU.max))
                sm(v.tensor_tensor_scan(backward[:, :, :].rearrange(flat)[:, ::-1], ab[:, ::-1], z[:, ::-1], -FAR,
                                        ALU.add, ALU.max))

            run_max(fwd, bwd)
            assert count[0] == 8
            for q, (column, source) in enumerate(((P - 1, dst_f), (0, dst_f), (P - 1, fwd), (0, bwd))):
                if q >= 2:
                    dve.wait_ge(s_sm_pe, q)
                sm(v.tensor_copy(spread[:, q % 2, :, :], source[:, :, column:column + 1].broadcast_to([HALF, 2, P])))
            dve.wait_ge(s_sm_pe, 5)
            sm(v.tensor_copy(tables[:, 0, :], bank[1][0:HALF, 0:2 * TILES]))
            sm(v.tensor_copy(tables[:, 1, :], bank[2][0:HALF, 0:2 * TILES]))
            for h in range(2):
                for column in (0, P - 1):
                    sm(v.tensor_scalar(pick[:, :], tables[:, 0, :], dst_f[:, h, column:column + 1], -FAR,
                                       ALU.not_equal, ALU.mult))
                    sm(v.tensor_tensor(pick[:, :], pick[:, :], tables[:, 1, :], ALU.add))
                    sm(v.tensor_reduce(best[:, :], pick[:, :], AX.X, ALU.max))
                    sm(v.tensor_tensor(zmax[:, h, (0 if column == 0 else 1):(1 if column == 0 else 2)],
                                       zr[:, h, column:column + 1], best[:, :], ALU.max))
            sm(v.tensor_copy(zkeep[:, :, :], zr[:, :, :]))
            sm(v.tensor_copy(zr[:, :, 0:1], zmax[:, :, 0:1]))
            sm(v.tensor_copy(zr[:, :, P - 1:P], zmax[:, :, 1:2]))
            run_max(fwd, bwd)
            sm(v.tensor_tensor(fwd[:, :, :], fwd[:, :, :], bwd[:, :, :], ALU.max))
            sm(v.tensor_tensor(row_a[:, :, :], zkeep[:, :, :], fwd[:, :, :], ALU.subtract))
            assert count[0] == SM_SHIFTED
            dve.wait_ge(s_sm_pe, 6)
            v.tensor_copy(cols[:, :, 1], bank[3][:, 0:TILES]).then_inc(s_cols, 1)
            dve.wait_ge(s_cols, 1)

            def selections(grp, rows_in, copied, built, used, weighted):
                g, b, n = grp
                wait(dve, used, ET * (g - 1))
                v.tensor_copy(colb[:, b, :, :], cols[:, bass.ds(g * ET, ET), :]).then_inc(copied, 1)
                dve.wait_ge(copied, g + 1)
                dve.wait_ge(rows_in[b], 16 * (n + 1))
                for j in range(ET):
                    row = drow[:, b, j * P:(j + 1) * P]
                    if weighted:
                        v.tensor_scalar(same[:, b, j, :], row, colb[:, b, j, 0:1], colb[:, b, j, 1:2],
                                        ALU.is_equal, ALU.mult).then_inc(built, 1)
                    else:
                        v.tensor_scalar(same[:, b, j, :], row, colb[:, b, j, 0:1], None,
                                        ALU.is_equal).then_inc(built, 1)
                    v.tensor_scalar(carry[:, b, j, :], row, colb[:, b, j, 2:3], None,
                                    ALU.is_equal).then_inc(built, 1)

            def select(grp):
                selections(grp, dr_in, s_cb, s_sel, s_ag, True)

            def finish_x1(grp):
                g, b, n = grp
                dve.wait_ge(s_age, ET * (g + 1))
                v.tensor_scalar(den[:, b, :], agg[:, b, :, D], 1e-30, None, ALU.max).then_inc(s_den, 1)
                dve.wait_ge(s_den, 2 * g + 1)
                v.reciprocal(rden[:, b, :], den[:, b, :]).then_inc(s_den, 1)
                dve.wait_ge(s_den, 2 * g + 2)
                for j in range(ET):
                    v.scalar_tensor_tensor(out=normed[:, b, j, :], in0=agg[:, b, j, 0:D], scalar=rden[:, b, j:j + 1],
                                           in1=mg[:, b, ET + j, 0:D], op0=ALU.mult, op1=ALU.add).then_inc(s_at, 1)
                dve.wait_ge(s_at, ET * (g + 1))
                if not (isinstance(g, int) and g < 2):
                    dve.wait_ge(scattered[b], 16 * ET * n)
                    dve.wait_ge(kept1[b], 16 * n)
                v.scalar_tensor_tensor(out=x1b[:, b, 0:ET, :].rearrange("p t d -> p (t d)"),
                                       in0=normed[:, b, 0:ET, :].rearrange("p t d -> p (t d)"), scalar=0.0,
                                       in1=xdst[:, bass.ds(g * EG, EG)], op0=ALU.max, op1=ALU.add).then_inc(s_xo, 1)

            for b in range(2):
                dve.wait_ge(kept[b], 16 * SLOT_USES[b])
                dve.wait_ge(x1_out[b], 16 * SLOT_USES[b])
            for b in range(2):
                dve.wait_ge(mg_in[b], 16)
            dve.wait_ge(s_zero, 3)

            def attend(at):
                stage(select, at(1))
                stage(finish_x1, at(0))

            staged(dve, GROUPS, -1, GROUPS - 1, attend)

            for b in range(2):
                dve.wait_ge(kept1[b], 16 * SLOT_USES[b])

            def take_moments_x1(grp):
                g, b, n = grp
                dve.wait_ge(gathered1[b], 16 * ET * (n + 1))
                moments(grp, s_stat1, s_mom1, ET,
                        lambda t: v.bn_stats(stats[:, b, t, :], xs[:, b, t, :]).then_inc(s_stat1, 1))

            def messages(grp):
                g, b, n = grp
                dve.wait_ge(s_f1, g + 1)
                dve.wait_ge(filt_in[b], 16 * (n + 1))
                wait(dve, s_tm, g)
                v.scalar_tensor_tensor(out=hT[:, 1, :], in0=filt[:, b, :], scalar=-LOG2, in1=bank[5][:, :],
                                       op0=ALU.add, op1=ALU.mult).then_inc(s_msg, 1)

            def add_sums(grp):
                g, b, n = grp
                dve.wait_ge(s_age1, ET * (g + 1))
                here = xdst[:, bass.ds(g * EG, EG)].rearrange("p (t d) -> p t d", d=D)
                v.tensor_tensor(here, here, agg[:, b, :, 0:D], ALU.add).then_inc(s_add1, 1)

            def convolve(at):
                stage(selections, at(0), dr_in1, s_cb1, s_sel1, s_ag1, False)
                stage(newton, at(1), s_guess1, s_newt1, ET)
                stage(messages, at(0))
                stage(take_moments_x1, at(2))
                stage(add_sums, at(-1))

            staged(dve, GROUPS, -2, GROUPS, convolve)


_INS = ["x", "src", "dst", "edge_attr_128", "L0_gnn_w", "L0_gnn_w_r", "L0_gnn_att_w", "L0_gnn_loop_w",
        "L1_gnn_fc1_w", "L1_gnn_w1", "L1_gnn_b1", "L1_gnn_w2", "L1_gnn_b2"]


def kernel(**inputs):
    import concourse.bacc as bacc
    import numpy as np
    from concourse.bass_utils import run_bass_kernel_spmd

    nc = bacc.Bacc("TRN2", target_bir_lowering=False, num_devices=1)
    arrays, args = {}, []
    for name in _INS:
        a = np.ascontiguousarray(inputs[name])
        arrays[f"in_{name}"] = a
        args.append(nc.dram_tensor(f"in_{name}", a.shape, mybir.dt.from_np(a.dtype), kind="ExternalInput").ap())
    out = nc.dram_tensor("out_x", inputs["x"].shape, F32, kind="ExternalOutput").ap()
    gnn_kernel(nc, *args, out)
    result = run_bass_kernel_spmd(nc, [arrays], core_ids=[0])
    return result.results[0]["out_x"]
```

```python
import math
from contextlib import ExitStack

import concourse.bass as bass
from concourse import mybir

ALU = mybir.AluOpType
ACT = mybir.ActivationFunctionType
AX = mybir.AxisListType
F32 = mybir.dt.float32
I32 = mybir.dt.int32
U16 = mybir.dt.uint16

P = 128
D = 128
DX = D + 1
ET = 4
NT = 8
LT = 2 * ET + NT
EPS = 1e-5
LOG2 = 0.6931471805599453
CAP = 40.0
EXP_CAP = math.exp(CAP)
FAR = 1e30
PAD_DST = 60000.0
SRC_ACT = 2
SRC_DVE = ET - SRC_ACT
NORM_ACT = SRC_ACT + NT
NORM_DVE = LT - NORM_ACT
SM_BCAST = 6
SM_SHIFTED = 5 + 4 + 2 + 16 + 3 + 2 + 2
SKIP = 100000.0


def wait(eng, sem, value):
    if not (isinstance(value, int) and value <= 0):
        eng.wait_ge(sem, value)


def wait_apart(eng, sem, value):
    wait(eng, sem, value)
    if not isinstance(value, int):
        eng.nop(nofuse=True)


UNROLL = 4


def staged(eng, groups, first, last, step, peeled=2):
    def of(k, c):
        def at(d):
            i = c + d
            number = UNROLL * k + i
            if isinstance(number, int) and not 0 <= number < groups:
                return None
            return number, i % 2, 2 * k + i // 2, i % 4, k + i // 4
        return at

    rounds = (groups - 5 - peeled) // UNROLL
    for i in range(first, peeled):
        step(of(0, i))
    with eng.Fori(0, rounds) as k:
        for c in range(peeled, peeled + UNROLL):
            step(of(k, c))
    for i in range(peeled + UNROLL * rounds, last + 1):
        step(of(0, i))


def stage(work, grp, *more):
    if grp is not None:
        work(grp, *more)


def gnn_kernel(nc, x, src, dst, ea, w, w_r, att_w, loop_w, fc1_w, w1, b1, w2, b2, out):
    N = x.shape[0]
    E = src.shape[0]
    TILES = -(-E // P)
    HALF = TILES // 2
    GROUPS = TILES // ET
    EG = ET * P
    NG = NT * P
    REST = E - (TILES - 1) * P
    assert TILES == 2 * HALF == ET * GROUPS and GROUPS % 2 == 1 and HALF <= P and 0 < REST < P
    assert (GROUPS - 1) * NG < N <= GROUPS * NG
    LAST_NODE = N - NG
    SLOT_USES = [len(range(b, GROUPS, 2)) for b in range(2)]
    SLOT4_USES = [len(range(q, GROUPS, 4)) for q in range(4)]

    ctx = ExitStack()
    with ctx:
        def sb(name, shape, dt=F32):
            return ctx.enter_context(nc.sbuf_tensor(name, shape, dt))

        def sem(name):
            return ctx.enter_context(nc.semaphore(name))

        def sem2(name):
            return [sem(f"{name}{b}") for b in range(2)]

        mg_dram = nc.dram_tensor("mg_scratch", [GROUPS, P, 2 * ET * DX], F32, kind="Internal").ap()
        mirror_dram = nc.dram_tensor("mirrored_dst", [TILES, P], U16, kind="Internal").ap()
        follow_dram = nc.dram_tensor("follows_tile_before", [TILES, P], F32, kind="Internal").ap()
        ea_dram = nc.dram_tensor("edge_attr_transposed", [GROUPS, P, EG], F32, kind="Internal").ap()
        filt_dram = nc.dram_tensor("filter_scratch", [GROUPS, P, EG], F32, kind="Internal").ap()

        ident = sb("ident", [P, P])
        wload = sb("wload", [P, 6, D])
        att = sb("att", [P, 3])
        loop_ext = sb("loop_ext", [P, DX])
        src_w = sb("src_w", [P, DX])
        rel_w = sb("rel_w", [P, DX])
        dst_w = sb("dst_w", [P, DX])
        fc1_t = sb("fc1_t", [P, D])
        w1_t = sb("w1_t", [P, D])
        w2_t = sb("w2_t", [P, D])
        b1_col = sb("b1_col", [P, 1])
        cap_b1 = sb("cap_b1", [P, 1])
        b2_col = sb("b2_col", [P, 1])
        b2_fold = sb("b2_fold", [P, 1])
        cap_b2 = sb("cap_b2", [P, 1])
        minus_log2 = sb("minus_log2", [P, P])

        xdst = sb("xdst", [P, TILES * D])
        score = sb("score", [P, 2, TILES])
        cols = sb("cols", [P, TILES, 2])
        gidx = sb("gidx", [P, GROUPS, 2 * ET], I32)
        sidx = sb("sidx", [P, TILES], I32)

        src_i = sb("src_i", [HALF, 2, P], I32)
        dst_i = sb("dst_i", [HALF, 2, P], I32)
        nxt_i = sb("nxt_i", [HALF, 2, P], I32)
        prev_i = sb("prev_i", [HALF, 2], I32)
        prev_f = sb("prev_f", [HALF, 2])
        mirrored = sb("mirrored", [HALF, 2, P], U16)
        follows = sb("follows", [HALF, 2, P])
        dst_f = sb("dst_f", [HALF, 2, P])
        row_a = sb("row_a", [HALF, 2, P])
        row_b = sb("row_b", [HALF, 2, P])

        xn = sb("xn", [P, 4, NT, D])
        xs = sb("xs", [P, 2, 2 * ET, D])
        eab = sb("eab", [P, 2, ET, D])
        normed = sb("normed", [P, 2, LT, D])
        hT = sb("hT", [P, 4, EG])
        mg = sb("mg", [P, 4, 2 * ET, DX])
        filt = sb("filt", [P, 2, EG])
        soft = sb("soft", [P, 3, EG])
        stats = sb("stats", [P, 2, LT, 6])
        msum = sb("msum", [P, 2, LT])
        mdif = sb("mdif", [P, 2, LT])
        var4 = sb("var4", [P, 2, LT])
        ln_v = sb("ln_v", [P, 2, LT])
        guess = sb("guess", [P, 2, LT])
        newt = sb("newt", [P, 2, LT])
        rstd = sb("rstd", [P, 2, LT])
        nmr = sb("nmr", [P, 2, LT])
        gix = sb("gix", [P, 2, 2, 2 * ET], I32)
        six = sb("six", [P, 2, 2, ET], I32)
        drow = sb("drow", [P, 2, EG], U16)
        colb = sb("colb", [P, 2, ET, 2])
        follow = xn[:, 2:4, ET:2 * ET, :]
        x1b = xn[:, 0:2, :, :]
        ends = sb("ends", [P, 2, ET, DX])
        den = sb("den", [P, 2, 2, 2])
        rden = sb("rden", [P, 2, 2, 2])
        fresh = soft[0:HALF, 1, 0:2 * P].rearrange("p (h e) -> p h e", h=2)
        fresh_back = soft[0:HALF, 1, 2 * P:4 * P].rearrange("p (h e) -> p h e", h=2)
        fwd = normed[0:HALF, 0, 4:6, :]
        bwd = normed[0:HALF, 0, 6:8, :]
        spread = normed[0:HALF, 0, 8:12, :].rearrange("p (q h) d -> p q h d", q=2)
        zkeep = normed[0:HALF, 0, 12:14, :]
        eps_col = sb("eps_col", [P, 1])
        zmax = sb("zmax", [HALF, 2, 2])
        best = sb("best", [HALF, 2])
        tables = hT[0:HALF, 0:2, 0:2 * TILES]
        pick = soft[0:HALF, 0, 0:2 * TILES].rearrange("p (k t) -> p k t", k=2)

        bank = [ctx.enter_context(nc.psum_tensor(f"bank{i}", [P, 512], F32)) for i in range(8)]
        TB, PB, NB = bank[0:2] + bank[6:8], bank[2:4], bank[4:6]
        WB = (bank[4], bank[6]), (bank[5], bank[7])

        def x1s(q, t):
            return xs[:, q % 2, (q // 2) * ET + t, :]

        def same(q):
            return xn[:, 2 + q, 0:ET, :] if q < 2 else eab[:, q - 2, :, :]

        def put_rows(q):
            return normed[:, q % 2, (1 + q // 2) * ET:(2 + q // 2) * ET, :]

        def sums_at(b, j, width, rows=slice(0, P)):
            return bank[2 * b + j % 2][rows, (j // 2) * DX:(j // 2) * DX + width]

        def sums_pair(b, par):
            return bank[2 * b + par][:, 0:2 * DX].rearrange("p (t d) -> p t d", d=DX)

        s_zero = sem("zeroed")
        s_ident = sem("ident_made")
        s_w = sem("weights_loaded")
        s_ends = sem("edge_ends_loaded")
        s_rows = sem("neighbour_rows_loaded")
        s_pads = sem("edge_rows_padded")
        s_pe0 = sem("setup_pe_done")
        s_dv0 = sem("setup_dve_done")
        s_col = sem("gather_index_steps")
        s_colpe = sem("gather_index_transposes")
        s_run = sem("run_table_steps")
        s_wready = sem("weights_ready")
        s_lw = sem("setup_copies")

        x_in = [sem(f"nodes_loaded{q}") for q in range(4)]
        ea_in = sem2("edge_attr_loaded")
        ea_out = sem2("transposed_edge_attr_stored")
        got_src = sem2("src_rows_gathered")
        got_dst = sem2("dst_rows_gathered")
        gix_set = sem("gather_index_set")
        kept = sem2("xdst_kept")
        s_stat = sem("stats_done")
        s_mom = sem("moment_steps")
        s_guess = sem("rstd_guessed")
        s_lnv = sem("ln_var_done")
        s_newt = sem("newton_steps")
        s_nd = sem("normed_by_dve")
        s_na = sem("normed_by_act")
        s_tp = sem("transposed")
        s_te = sem("transposes_evicted")
        s_mg = sem("mg_products")
        s_mge = sem("mg_evicted")
        s_w1 = sem("filter1_product")
        s_w2 = sem("filter2_product")
        s_p1 = sem("filter1_act_steps")
        s_p2 = sem("filter2_act_steps")
        s_sp1 = sem("filter1_done")
        s_sp2 = sem("filter2_done")
        s_nh = sem("node_products")
        s_x1 = sem("nodes_combined")
        s_z = sem("score_steps")
        x1_out = [sem(f"nodes_stored{q}") for q in range(4)]
        mg_out = sem2("mg_stored")
        filt_out = sem2("filter_stored")

        s_sm_pe = sem("softmax_pe")
        s_sm_dve = sem("softmax_dve")
        s_sm_act = sem("softmax_act")
        s_cols = sem("softmax_done")
        s_tabs = sem("run_tables_stored")
        s_clear = sem("cleared")
        fo_in = sem2("follows_loaded")
        fo_in1 = sem2("follows_loaded_1")

        mg_in = [sem(f"mg_loaded{q}") for q in range(4)]
        dr_in = sem2("dst_rows_loaded")
        et_in = sem2("transposed_edge_attr_loaded")
        s_cb = sem("columns_copied")
        s_sel = sem("selections_built")
        s_ag = sem("sums_product")
        s_age = sem("sums_evicted")
        s_den = sem("weights_inverted")
        s_at = sem("attended")
        s_xo = sem("x1_rows_done")
        six_set = sem("scatter_index_set")
        scattered = sem2("x1_scattered")
        kept1 = sem2("x1_kept")

        gathered1 = [sem(f"x1_gathered{q}") for q in range(4)]
        gix_set1 = sem("gather_index_set_1")
        filt_in = sem2("filter_loaded")
        dr_in1 = sem2("dst_rows_loaded_1")
        s_stat1 = sem("stats_done_1")
        s_mom1 = sem("moment_steps_1")
        s_lnv1 = sem("ln_var_done_1")
        s_guess1 = sem("rstd_guessed_1")
        s_newt1 = sem("newton_steps_1")
        s_n1 = sem("normed_1")
        s_tp1 = sem("transposed_1")
        s_te1 = sem("transposes_evicted_1")
        s_f1 = sem("fc1_product")
        s_msg = sem("messages_done")
        s_tm = sem("messages_transposed")
        s_me = sem("messages_evicted")
        s_cb1 = sem("columns_copied_1")
        s_sel1 = sem("selections_built_1")
        s_ag1 = sem("sums_product_1")
        s_age1 = sem("sums_evicted_1")
        s_add1 = sem("sums_added_1")
        s_buf = sem("rows_buffered")
        six_set1 = sem("scatter_index_set_1")
        put = [sem(f"out_scattered{q}") for q in range(4)]

        block = ctx.enter_context(nc.Block())

        @block.sync
        def _(sp):
            sp.wait_ge(s_pads, 4)
            h1 = HALF * P
            full = (TILES - 1) * P

            def load_rows_of(tile, a, off, rest, loaded):
                sp.dma_start(tile[:, 0, :], a[off:off + h1].rearrange("(t p) -> t p", p=P)).then_inc(loaded, 16)
                sp.dma_start(tile[0:HALF - 1, 1, :],
                             a[off + h1:off + full].rearrange("(t p) -> t p", p=P)).then_inc(loaded, 16)
                sp.dma_start(tile[HALF - 1:HALF, 1, 0:rest],
                             a[off + full:E].rearrange("(a n) -> a n", a=1)).then_inc(loaded, 16)

            load_rows_of(src_i, src, 0, REST, s_ends)
            load_rows_of(dst_i, dst, 0, REST, s_ends)
            for n, a in enumerate((w, w_r, loop_w, fc1_w, w1, w2)):
                sp.dma_start(wload[:, n, :], a).then_inc(s_w, 16)
            sp.dma_start(att[:, :], att_w.rearrange("(t p) -> p t", p=P),
                         allow_slow_non_contiguous=True).then_inc(s_w, 16)
            sp.dma_start(b1_col[:, :], b1.rearrange("(p a) -> p a", a=1)).then_inc(s_w, 16)
            sp.dma_start(b2_col[:, :], b2.rearrange("(p a) -> p a", a=1)).then_inc(s_w, 16)
            load_rows_of(nxt_i, dst, 1, REST - 1, s_rows)
            for half, p0, first, rows in ((0, 1, P - 1, HALF - 1), (1, 0, h1 - 1, HALF - 1), (1, HALF - 1, full - 1, 1)):
                a = dst[first:first + rows * P] if rows > 1 else dst[first:first + 1]
                sp.dma_start(prev_i[p0:p0 + rows, half:half + 1],
                             a.rearrange("(t p) -> t p", t=rows)[:, 0:1],
                             allow_slow_non_contiguous=True).then_inc(s_rows, 16)

            def store_tables():
                sp.wait_ge(s_run, 6)
                for half in range(2):
                    tiles = slice(half * HALF, (half + 1) * HALF)
                    sp.dma_start(mirror_dram[tiles, :], mirrored[:, half, :]).then_inc(s_tabs, 16)
                    sp.dma_start(follow_dram[tiles, :], follows[:, half, :]).then_inc(s_tabs, 16)

            def load_nodes(grp):
                g, b, n, q, m = grp
                wait_apart(sp, x1_out[q], 16 * m)
                start = LAST_NODE if isinstance(g, int) and g == GROUPS - 1 else g * NG
                sp.dma_start(xn[:, q, :, :].rearrange("p t d -> p (t d)"),
                             x[bass.ds(start, NG), :].rearrange("(p t) d -> p (t d)", p=P)).then_inc(x_in[q], 16)

            def load_edges(grp):
                g, b, n, q, m = grp
                final = isinstance(g, int) and g == GROUPS - 1
                if isinstance(g, int) and g == 0:
                    sp.wait_ge(s_zero, 1)
                wait_apart(sp, s_tp, 5 * g - 7)
                tiles = ET - 1 if final else ET
                sp.dma_start(eab[:, b, 0:tiles, :], ea[bass.ds(g * EG, tiles * P), :]
                             .rearrange("(t p) d -> p t d", p=P)).then_inc(ea_in[b], 16)
                if final:
                    sp.dma_start(eab[0:REST, b, ET - 1, :], ea[E - REST:E, :]).then_inc(ea_in[b], 16)

            def keep_dst(grp):
                g, b, n, q, m = grp
                wait_apart(sp, got_dst[b], 16 * ET * (n + 1))
                sp.dma_start(xdst[:, bass.ds(g * EG, EG)],
                             xs[:, b, ET:2 * ET, :].rearrange("p t d -> p (t d)")).then_inc(kept[b], 16)

            def store_nodes(grp):
                g, b, n, q, m = grp
                wait_apart(sp, s_x1, 2 * (g + 1))
                start = g * NG
                if isinstance(g, int) and g == GROUPS - 1:
                    start = LAST_NODE
                    for c in range(4):
                        sp.wait_ge(x1_out[c], 16 * (SLOT4_USES[c] - (c == q)))
                sp.dma_start(out[bass.ds(start, NG), :].rearrange("(p t) d -> p (t d)", p=P),
                             xn[:, q, :, :].rearrange("p t d -> p (t d)")).then_inc(x1_out[q], 16)

            def store_mg(grp):
                g, b, n, q, m = grp
                wait_apart(sp, s_z, 2 * (g + 1))
                sp.dma_start(mg_dram[g], mg[:, b, :, :].rearrange("p t d -> p (t d)")).then_inc(mg_out[b], 16)

            def store_ea(grp):
                g, b, n, q, m = grp
                wait_apart(sp, s_te, 5 * g + 3)
                sp.dma_start(ea_dram[g], filt[:, b, :]).then_inc(ea_out[b], 16)

            def node_and_edge(at):
                stage(store_ea, at(-1))
                stage(store_nodes, at(-1))
                stage(store_mg, at(-1))
                stage(keep_dst, at(2))
                stage(load_edges, at(2))
                stage(load_nodes, at(3))

            staged(sp, GROUPS, -3, GROUPS, node_and_edge)
            store_tables()
            sp.wait_ge(s_tabs, 64)
            sp.wait_ge(s_clear, 1)

            for b in range(2):
                sp.wait_ge(mg_out[b], 16 * SLOT_USES[b])
                sp.wait_ge(ea_out[b], 16 * SLOT_USES[b])

            def load_ea(grp):
                g, b, n, q, m = grp
                wait_apart(sp, s_w1, g - 1)
                sp.dma_start(hT[:, 2 + b, :], ea_dram[g]).then_inc(et_in[b], 16)

            def store_filter(grp):
                g, b, n, q, m = grp
                wait_apart(sp, s_sp2, g + 1)
                sp.dma_start(filt_dram[g], filt[:, b, :]).then_inc(filt_out[b], 16)

            def load_rows(grp, built, rows_in):
                g, b, n, q, m = grp
                wait_apart(sp, built, ET * (g - 1))
                sp.dma_start(drow[:, b, :], mirror_dram[bass.ds(g * ET, ET), :].rearrange("(a t) p -> a (t p)", a=1)
                             .partition_broadcast(P)).then_inc(rows_in[b], 16)

            def load_follows(grp, summed, follow_in):
                g, b, n, q, m = grp
                wait_apart(sp, summed, ET * (g - 1))
                sp.dma_start(follow[0:1, b, :, :].rearrange("p t e -> p (t e)"),
                             follow_dram[bass.ds(g * ET, ET), :].rearrange("(a t) p -> a (t p)", a=1)
                             ).then_inc(follow_in[b], 16)

            def load_mg(grp):
                g, b, n, q, m = grp
                wait_apart(sp, s_at, ET * (g - 3))
                sp.dma_start(mg[:, q, :, :].rearrange("p t d -> p (t d)"), mg_dram[g]).then_inc(mg_in[q], 16)

            def keep_x1(grp):
                g, b, n, q, m = grp
                wait_apart(sp, s_xo, g + 1)
                sp.dma_start(xdst[:, bass.ds(g * EG, EG)],
                             x1b[:, b, 0:ET, :].rearrange("p t d -> p (t d)")).then_inc(kept1[b], 16)

            def attend(at):
                stage(load_follows, at(1), s_ag, fo_in)
                stage(load_rows, at(3), s_sel, dr_in)
                stage(load_mg, at(2))
                stage(load_ea, at(1))
                stage(store_filter, at(-3))
                stage(keep_x1, at(-1))

            staged(sp, GROUPS, -3, GROUPS + 2, attend, 3)

            for b in range(2):
                sp.wait_ge(filt_out[b], 16 * SLOT_USES[b])
            sp.wait_ge(s_sel, ET * GROUPS)
            sp.wait_ge(s_ag, ET * GROUPS)

            def load_filter(grp):
                g, b, n, q, m = grp
                wait_apart(sp, s_msg, g - 1)
                sp.dma_start(filt[:, b, :], filt_dram[g]).then_inc(filt_in[b], 16)

            def convolve(at):
                stage(load_rows, at(0), s_sel1, dr_in1)
                stage(load_follows, at(-1), s_ag1, fo_in1)
                stage(load_filter, at(1))

            staged(sp, GROUPS, -2, GROUPS, convolve)
            for c in range(4):
                sp.wait_ge(put[c], 16 * ET * SLOT4_USES[c])

        @block.gpsimd
        def _(pool):
            nc.gpsimd.memset(src_i[:, :, :], 0).then_inc(s_pads, 1)
            nc.gpsimd.memset(dst_i[:, :, :], int(PAD_DST)).then_inc(s_pads, 1)
            nc.gpsimd.memset(nxt_i[:, :, :], int(PAD_DST)).then_inc(s_pads, 1)
            nc.gpsimd.memset(prev_i[:, :], -1).then_inc(s_pads, 1)
            nc.gpsimd.memset(ident[:, :], 0.0).then_inc(s_ident, 1)
            pool.wait_ge(s_ident, 1)
            nc.gpsimd.affine_select(out=ident[:, :], in_=ident[:, :], compare_op=ALU.not_equal, fill=1.0,
                                    base=0, pattern=[[-1, P]], channel_multiplier=1).then_inc(s_ident, 1)
            nc.gpsimd.memset(minus_log2[:, :], -LOG2).then_inc(s_ident, 1)
            nc.gpsimd.memset(eab[:, :, :, :], 0.0).then_inc(s_zero, 1)
            nc.gpsimd.memset(ends[:, :, :, :], 0.0).then_inc(s_zero, 1)

            pool.wait_ge(s_col, 5)

            def first_indices(buffer, kept_indices, copied):
                nc.gpsimd.tensor_copy(buffer[:, 0, :, :], kept_indices[:, 0:2, :]).then_inc(copied, 1)

            def next_indices(grp, buffer, kept_indices, copied):
                g, b, n, q, m = grp
                two = 1 if isinstance(g, int) and g + 2 >= GROUPS else 2
                nc.gpsimd.tensor_copy(buffer[:, 1 - q // 2, 0:two, :],
                                      kept_indices[:, bass.ds(g + 1, two), :]).then_inc(copied, 1)

            def gather(grp):
                g, b, n, q, m = grp
                if b == 1:
                    for c in range(2):
                        wait(pool, got_src[c], 16 * ET * n)
                        wait_apart(pool, got_dst[c], 16 * ET * n)
                    next_indices(grp, gix, gidx, gix_set)
                wait_apart(pool, gix_set, n + 1)
                for t in range(2 * ET):
                    if t % ET == 0:
                        wait_apart(pool, s_nd, NORM_DVE * g - 2 * NORM_DVE + t + SRC_DVE)
                    if t == 0:
                        wait_apart(pool, s_na, NORM_ACT * g - 2 * NORM_ACT + SRC_ACT)
                    if t == ET:
                        wait_apart(pool, kept[b], 16 * n)
                    pool.indirect_dma_start(xs[:, b, t, :], None, x, bass.IndirectOffsetOnAxis(gix[:, q // 2, b, t:t + 1], 0)
                                            ).then_inc(got_src[b] if t < ET else got_dst[b], 16)

            first_indices(gix, gidx, gix_set)
            staged(pool, GROUPS, 0, GROUPS - 1, lambda at: gather(at(0)))

            for c in range(4):
                pool.wait_ge(x1_out[c], 16 * SLOT4_USES[c])
            nc.gpsimd.memset(follow, 0.0).then_inc(s_clear, 1)

            sidx_groups = sidx[:, :].rearrange("p (g t) -> p g t", t=ET)

            def scatter(grp, done, index_set, data):
                g, b, n, q, m = grp
                slot = b if done is scattered else q
                rows = x1b[:, b, 0:ET, :] if done is scattered else put_rows(q)
                if b == 1:
                    for c in range(2):
                        if done is scattered:
                            wait_apart(pool, done[c], 16 * ET * n)
                        else:
                            wait_apart(pool, done[(q + 1) % 4 + c], 16 * ET * (m + q // 2))
                    next_indices(grp, six, sidx_groups, index_set)
                wait_apart(pool, index_set, n + 1)
                wait_apart(pool, data, g + 1)
                for t in range(ET):
                    pool.indirect_dma_start(out, bass.IndirectOffsetOnAxis(six[:, q // 2, b, t:t + 1], 0), rows[:, t, :],
                                            None, bounds_check=N - 1, oob_is_err=False).then_inc(done[slot], 16)

            pool.wait_ge(s_run, 12)
            first_indices(six, sidx_groups, six_set)
            staged(pool, GROUPS, 0, GROUPS - 1, lambda at: scatter(at(0), scattered, six_set, s_xo))

            for b in range(2):
                pool.wait_ge(scattered[b], 16 * ET * SLOT_USES[b])

            again, src_groups = gix[:, :, :, 0:ET], gidx[:, :, 0:ET]
            first_indices(again, src_groups, gix_set1)

            def gather_again(grp):
                g, b, n, q, m = grp
                if b == 1:
                    for c in range(2):
                        wait_apart(pool, gathered1[(q + 1) % 4 + c], 16 * ET * (m + q // 2))
                    next_indices(grp, again, src_groups, gix_set1)
                wait_apart(pool, gix_set1, n + 1)
                wait_apart(pool, s_n1, ET * (g - 3))
                for t in range(ET):
                    pool.indirect_dma_start(x1s(q, t), None, out,
                                            bass.IndirectOffsetOnAxis(gix[:, q // 2, b, t:t + 1], 0)).then_inc(gathered1[q], 16)

            staged(pool, GROUPS, 0, GROUPS - 1, lambda at: gather_again(at(0)), 3)

            for c in range(4):
                pool.wait_ge(gathered1[c], 16 * ET * SLOT4_USES[c])
            first_indices(six, sidx_groups, six_set1)
            staged(pool, GROUPS, 0, GROUPS - 1, lambda at: scatter(at(0), put, six_set1, s_buf))
            for c in range(4):
                pool.wait_ge(put[c], 16 * ET * SLOT4_USES[c])

        @block.tensor
        def _(pe):
            def turn_rows(rows, psum, turned):
                for h in range(2):
                    last = pe.transpose(psum[:, h * HALF:(h + 1) * HALF], rows[:, h, :], ident[0:HALF, 0:HALF])
                last.then_inc(turned, 1)

            pe.wait_ge(s_ident, 3)
            pe.wait_ge(s_col, 1)
            turn_rows(row_a, bank[4], s_colpe)
            pe.wait_ge(s_col, 3)
            turn_rows(row_b, bank[5], s_colpe)
            pe.wait_ge(s_w, 16 * 9)
            for n, i in enumerate((0, 1, 3, 4)):
                last = pe.transpose(bank[0][:, n * D:(n + 1) * D], wload[:, i, :], ident[:, :])
            last.then_inc(s_pe0, 1)
            pe.transpose(bank[1][:, 0:D], wload[:, 5, :], ident[:, :]).then_inc(s_pe0, 1)
            pe.wait_ge(s_dv0, 1)
            pe.matmul(bank[2][:, 0:DX], wload[:, 0, :], loop_ext[:, :], start=True, stop=True)
            pe.matmul(bank[2][:, 256:257], wload[:, 0, :], att[:, 0:1], start=True, stop=True)
            pe.matmul(bank[2][:, 260:261], wload[:, 1, :], att[:, 2:3], start=True, stop=True).then_inc(s_pe0, 1)
            pe.wait_ge(s_dv0, 3)
            pe.matmul(bank[3][:, 0:1], w2_t[:, :], minus_log2[:, 0:1], start=True, stop=True).then_inc(s_pe0, 1)
            pe.wait_ge(s_wready, 1)

            def transposes(grp, i, source):
                g, b, n, q, m = grp
                wait(pe, s_te, 5 * g + i - 3)
                for t in range(ET):
                    last = pe.transpose(TB[(q + i) % 4][:, t * P:(t + 1) * P], source(t), ident[:, :])
                last.then_inc(s_tp, 1)

            def pair(grp, lo, r):
                g, b, n, q, m = grp
                wait(pe, s_mge, 4 * g + r - 1)
                psum = PB[r % 2]
                for t in range(lo, lo + 2):
                    o = psum[:, (t - lo) * DX:(t - lo + 1) * DX]
                    tile = slice(t * P, (t + 1) * P)
                    if r % 2 == 0:
                        last = pe.matmul(o, hT[:, 1, tile], dst_w[:, :], start=True, stop=True)
                    else:
                        pe.matmul(o, hT[:, 0, tile], src_w[:, :], start=True, stop=False)
                        last = pe.matmul(o, filt[:, b, tile], rel_w[:, :], start=False, stop=True)
                last.then_inc(s_mg, 1)

            def node_half(grp, half):
                g, b, n, q, m = grp
                pe.wait_ge(s_te, 5 * g + 4 + half)
                wait(pe, s_x1, 2 * g - 1 + half)
                for t in range(4):
                    last = pe.matmul(NB[half][:, t * D:(t + 1) * D], hT[:, 2 + half, t * P:(t + 1) * P],
                                     src_w[:, 0:D], start=True, stop=True)
                last.then_inc(s_nh, 1)

            def node_and_edge(at):
                grp = at(0)
                g, b, n, q, m = grp
                pe.wait_ge(s_nd, NORM_DVE * g + SRC_DVE)
                pe.wait_ge(s_na, NORM_ACT * g + SRC_ACT)
                transposes(grp, 0, lambda t: normed[:, b, NT + t, :])
                pe.wait_ge(s_nd, NORM_DVE * (g + 1))
                transposes(grp, 1, lambda t: normed[:, b, NT + ET + t, :])
                pe.wait_ge(ea_in[b], 16 * (n + 1) + (16 if isinstance(g, int) and g == GROUPS - 1 else 0))
                transposes(grp, 2, lambda t: eab[:, b, t, :])
                pe.wait_ge(s_na, NORM_ACT * (g + 1))
                transposes(grp, 3, lambda t: normed[:, b, t, :])
                pe.wait_ge(s_te, 5 * g + 2)
                pair(grp, 0, 0)
                transposes(grp, 4, lambda t: normed[:, b, 4 + t, :])
                pe.wait_ge(s_te, 5 * g + 3)
                pair(grp, 0, 1)
                pair(grp, 2, 2)
                node_half(grp, 0)
                pair(grp, 2, 3)
                node_half(grp, 1)

            staged(pe, GROUPS, 0, GROUPS - 1, node_and_edge)

            pe.wait_ge(s_te, 5 * GROUPS)
            pe.wait_ge(s_run, 3)
            turn_rows(row_a, bank[6], s_pe0)
            turn_rows(dst_f, bank[7], s_pe0)

            pe.wait_ge(s_z, 2 * GROUPS)
            pe.wait_ge(s_te, 5 * GROUPS)
            for part in range(2):
                for h in range(2):
                    o = (2 * part + h) * P
                    last = pe.transpose(bank[0][0:HALF, o:o + P], score[:, part, h * HALF:(h + 1) * HALF], ident[:, :])
            last.then_inc(s_sm_pe, 1)
            for q in range(4):
                pe.wait_ge(s_sm_dve, SM_BCAST + q)
                for h in range(2):
                    last = pe.transpose(bank[1 + q // 2][:, (q % 2) * TILES + h * HALF:(q % 2) * TILES + (h + 1) * HALF],
                                        spread[:, q % 2, h, :], ident[0:HALF, 0:HALF])
                last.then_inc(s_sm_pe, 1)
            pe.wait_ge(s_sm_act, 1)
            for h in range(2):
                last = pe.transpose(bank[3][:, h * HALF:(h + 1) * HALF], row_b[:, h, :], ident[0:HALF, 0:HALF])
            last.then_inc(s_sm_pe, 1)

            def own(grp, j, rows, width, selected, freed, per):
                g, b, n, q, m = grp
                pe.wait_ge(selected, ET * g + j + 1)
                if j == 0:
                    wait(pe, freed, per * (g - 1))
                pe.matmul(sums_at(b, j, width), same(q)[:, j, :], rows, start=True, stop=False)

            def carried(grp, j, width, evicted, made):
                g, b, n, q, m = grp
                wait(pe, evicted, ET * g + j)
                before = ends[:, b, j - 1, 0:width] if j else ends[:, 1 - b, ET - 1, 0:width]
                pe.matmul(sums_at(b, j, width), follow[:, b, j, :], before, start=False, stop=True).then_inc(made, 1)

            def own_rows(grp, j):
                g, b, n, q, m = grp
                if j == 0:
                    pe.wait_ge(mg_in[q], 16 * (m + 1))
                own(grp, j, mg[:, q, j, :], DX, s_sel, s_at, ET)

            def carried_rows(grp, j):
                g, b, n, q, m = grp
                if j == 0:
                    pe.wait_ge(fo_in[b], 16 * (n + 1))
                carried(grp, j, DX, s_age, s_ag)

            def first_filter(grp):
                g, b, n, q, m = grp
                pe.wait_ge(et_in[b], 16 * (n + 1))
                wait(pe, s_sp1, g - 1)
                pe.matmul(WB[0][b][:, :], w1_t[:, :], hT[:, 2 + b, :], start=True, stop=True).then_inc(s_w1, 1)

            def second_filter(grp):
                g, b, n, q, m = grp
                pe.wait_ge(s_sp1, g + 1)
                wait(pe, s_sp2, g - 1)
                pe.matmul(WB[1][b][:, :], w2_t[:, :], soft[:, 2, :], start=True, stop=True).then_inc(s_w2, 1)

            def attend(at):
                stage(carried_rows, at(0), 0)
                stage(carried_rows, at(0), 1)
                stage(own_rows, at(0), 2)
                stage(first_filter, at(-1))
                stage(carried_rows, at(0), 2)
                stage(own_rows, at(0), 3)
                stage(carried_rows, at(0), 3)
                stage(own_rows, at(1), 0)
                stage(own_rows, at(1), 1)
                stage(second_filter, at(-2))

            pe.wait_ge(s_cols, 1)
            pe.wait_ge(s_zero, 2)
            pe.wait_ge(s_x1, 2 * GROUPS)
            staged(pe, GROUPS, -1, GROUPS + 1, attend, 3)

            pe.wait_ge(s_xo, GROUPS)
            pe.wait_ge(s_sp2, GROUPS)

            def turn_x1(grp):
                g, b, n, q, m = grp
                pe.wait_ge(s_n1, ET * (g + 1))
                wait(pe, s_te1, g)
                for t in range(ET):
                    last = pe.transpose(bank[4][:, t * P:(t + 1) * P], normed[:, b, t, :], ident[:, :])
                last.then_inc(s_tp1, 1)

            def project(grp):
                g, b, n, q, m = grp
                pe.wait_ge(s_te1, g + 1)
                wait(pe, s_msg, g)
                pe.matmul(bank[5][:, :], fc1_t[:, :], hT[:, 0, :], start=True, stop=True).then_inc(s_f1, 1)

            def turn_messages(grp):
                g, b, n, q, m = grp
                pe.wait_ge(s_msg, g + 1)
                wait(pe, s_me, g)
                for t in range(ET):
                    last = pe.transpose(bank[6][:, t * P:(t + 1) * P], hT[:, 1, t * P:(t + 1) * P], ident[:, :])
                last.then_inc(s_tm, 1)

            def sum_tile(grp, j, part):
                g, b, n, q, m = grp
                if part == 0:
                    if j == 0:
                        pe.wait_ge(s_me, g + 1)
                    own(grp, j, x1b[:, b, ET + j, :], D, s_sel1, s_add1, 2)
                else:
                    if j == 0:
                        pe.wait_ge(fo_in1[b], 16 * (n + 1))
                    carried(grp, j, D, s_age1, s_ag1)

            def convolve(at):
                stage(sum_tile, at(-3), 0, 1)
                stage(turn_x1, at(0))
                stage(sum_tile, at(-3), 1, 1)
                stage(sum_tile, at(-3), 2, 0)
                stage(sum_tile, at(-3), 2, 1)
                stage(project, at(0))
                stage(sum_tile, at(-3), 3, 0)
                stage(sum_tile, at(-3), 3, 1)
                stage(turn_messages, at(-1))
                stage(sum_tile, at(-2), 0, 0)
                stage(sum_tile, at(-2), 1, 0)

            staged(pe, GROUPS, 0, GROUPS + 2, convolve, 3)

        @block.scalar
        def _(act):
            act.preload_act_table_set("natural_log_exp_and_others")

            def guess_rstd(grp, moments, ln_done, guessed, lt):
                g, b, n, q, m = grp
                act.wait_ge(moments, 5 * (g + 1))
                act.activation(ln_v[:, b, 0:lt], var4[:, b, 0:lt], ACT.Ln, scale=0.25, bias=eps_col[:, 0:1]).then_inc(ln_done, 1)
                act.wait_ge(ln_done, g + 1)
                act.activation(guess[:, b, 0:lt], ln_v[:, b, 0:lt], ACT.Exp, scale=-0.5).then_inc(guessed, 1)

            def normalize(grp, lo):
                g, b, n, q, m = grp
                act.wait_ge(s_newt, 5 * (g + 1))
                wait(act, s_tp, 5 * (g - 1))
                for i in range(lo, lo + NORM_ACT // 2):
                    t = NT + i if i < SRC_ACT else i - SRC_ACT
                    act.activation(normed[:, b, t, :], xn[:, q, t, :] if t < NT else xs[:, b, t - NT, :], ACT.Identity,
                                   bias=nmr[:, b, t:t + 1], scale=rstd[:, b, t:t + 1]).then_inc(s_na, 1)

            def evict(grp, i):
                g, b, n, q, m = grp
                act.wait_ge(s_tp, 5 * g + i + 1)
                if i < 3:
                    wait(act, s_mg, 4 * g)
                else:
                    wait(act, s_nh, 2 * g - 4 + i)
                if i == 2:
                    wait(act, ea_out[b], 16 * n)
                to = (hT[:, 0, :], hT[:, 1, :], filt[:, b, :], hT[:, 2, :], hT[:, 3, :])[i]
                act.activation(to, TB[(q + i) % 4][:, :], ACT.Copy if i == 2 else ACT.Relu).then_inc(s_te, 1)

            def evict_pair(grp, r):
                g, b, n, q, m = grp
                act.wait_ge(s_mg, 4 * g + r + 1)
                if r == 0:
                    wait(act, mg_out[b], 16 * n)
                lo = (r // 2) * 2 + (ET if r % 2 == 0 else 0)
                act.copy(mg[:, b, lo:lo + 2, :].rearrange("p t d -> p (t d)"), PB[r % 2][:, 0:2 * DX]).then_inc(s_mge, 1)

            def softplus_step(grp, layer, k):
                g, b, n, q, m = grp
                buf, steps, used = soft[:, layer, :], (s_p1, s_p2)[layer], (s_sp1, s_sp2)[layer]
                if k == 0:
                    act.wait_ge((s_w1, s_w2)[layer], g + 1)
                    wait(act, used, g)
                    act.activation(buf, WB[layer][b][:, :], ACT.Relu, scale=-1.0,
                                   bias=(cap_b1, cap_b2)[layer][:, 0:1]).then_inc(steps, 1)
                    return
                act.wait_ge(steps, 3 * g + k)
                if k == 1:
                    act.activation(buf, buf, ACT.Exp, scale=-1.0).then_inc(steps, 1)
                else:
                    act.activation(buf, buf, ACT.Ln, scale=EXP_CAP, bias=1.0).then_inc(steps, 1)

            def node_and_edge(at):
                stage(evict, at(0), 0)
                stage(evict, at(0), 1)
                stage(evict, at(0), 2)
                stage(evict, at(0), 3)
                stage(normalize, at(1), 0)
                stage(evict_pair, at(0), 0)
                stage(evict_pair, at(0), 1)
                stage(evict, at(0), 4)
                stage(normalize, at(1), NORM_ACT // 2)
                stage(evict_pair, at(0), 2)
                stage(evict_pair, at(0), 3)
                stage(guess_rstd, at(2), s_mom, s_lnv, s_guess, LT)

            act.wait_ge(s_wready, 1)
            staged(act, GROUPS, -2, GROUPS - 1, node_and_edge)

            act.wait_ge(s_sm_dve, SM_SHIFTED)
            act.activation(row_b[:, :, :], row_a[:, :, :], ACT.Exp).then_inc(s_sm_act, 1)

            def evict_end(grp, j, width, ready, evicted):
                g, b, n, q, m = grp
                act.wait_ge(ready, ET * g + j + 1)
                act.copy(ends[0:1, b, j, 0:width], sums_at(b, j, width, slice(0, 1))).then_inc(evicted, 1)

            def attend(at):
                stage(evict_end, at(0), 0, DX, s_ag, s_age)
                stage(softplus_step, at(-3), 1, 0)
                stage(evict_end, at(0), 1, DX, s_ag, s_age)
                stage(softplus_step, at(-3), 1, 1)
                stage(softplus_step, at(-3), 1, 2)
                stage(evict_end, at(0), 2, DX, s_ag, s_age)
                stage(softplus_step, at(-1), 0, 0)
                stage(softplus_step, at(-1), 0, 1)
                stage(evict_end, at(0), 3, DX, s_ag, s_age)
                stage(softplus_step, at(-1), 0, 2)

            act.wait_ge(s_zero, 2)
            staged(act, GROUPS, 0, GROUPS + 2, attend, 3)

            def normalize_x1(grp, lo):
                g, b, n, q, m = grp
                if lo == 0:
                    act.wait_ge(s_newt1, 5 * (g + 1))
                    wait(act, s_tp1, g - 1)
                for t in range(lo, lo + 2):
                    act.activation(normed[:, b, t, :], x1s(q, t), ACT.Identity,
                                   bias=nmr[:, b, t:t + 1], scale=rstd[:, b, t:t + 1]).then_inc(s_n1, 1)

            def evict_x1(grp):
                g, b, n, q, m = grp
                act.wait_ge(s_tp1, g + 1)
                wait(act, s_f1, g)
                act.activation(hT[:, 0, :], bank[4][:, :], ACT.Relu).then_inc(s_te1, 1)

            def evict_messages(grp):
                g, b, n, q, m = grp
                act.wait_ge(s_tm, g + 1)
                wait(act, s_ag1, ET * (g - 1))
                act.copy(x1b[:, b, ET:2 * ET, :].rearrange("p t d -> p (t d)"), bank[6][:, :]).then_inc(s_me, 1)

            def convolve(at):
                def sums(j):
                    stage(evict_end, at(-3), j, D, s_ag1, s_age1)

                sums(0)
                stage(evict_x1, at(0))
                sums(1)
                stage(normalize_x1, at(1), 0)
                sums(2)
                stage(normalize_x1, at(1), 2)
                sums(3)
                stage(guess_rstd, at(2), s_mom1, s_lnv1, s_guess1, ET)
                stage(evict_messages, at(-1))
                if at(5) is None:
                    buffer_rows((early[0], early[0] % 2, early[0] // 2, early[0] % 4, early[0] // 4))
                    early[0] += 1

            def buffer_rows(grp):
                g, b, n, q, m = grp
                wait(act, put[q], 16 * ET * m)
                act.wait_ge(s_add1, 2 * (g + 1))
                act.copy(put_rows(q), xdst[:, bass.ds(g * EG, EG)].rearrange("p (t d) -> p t d", d=D)).then_inc(s_buf, 1)

            act.wait_ge(s_at, ET * GROUPS)
            early = [0]
            staged(act, GROUPS, -2, GROUPS + 2, convolve, 3)
            staged(act, GROUPS, early[0], GROUPS - 1, lambda at: buffer_rows(at(0)), early[0])

        @block.vector
        def _(dve):
            v = nc.vector
            made = [0]

            def index_step(ins):
                made[0] += 1
                ins.then_inc(s_col, 1)
                dve.wait_ge(s_col, made[0])

            def in_groups(psum):
                return psum[:, 0:TILES].rearrange("p (g t) -> p g t", t=ET)

            dve.wait_ge(s_ends, 16 * 6)
            index_step(v.tensor_copy(row_a[:, :, :], src_i[:, :, :]))
            index_step(v.tensor_copy(dst_f[:, :, :], dst_i[:, :, :]))
            index_step(v.tensor_scalar(row_b[:, :, :], dst_f[:, :, ::-1], float(N - 1), None, ALU.min))
            dve.wait_ge(s_colpe, 1)
            index_step(v.tensor_copy(gidx[:, :, 0:ET], in_groups(bank[4])))
            dve.wait_ge(s_colpe, 2)
            index_step(v.tensor_copy(gidx[:, :, ET:2 * ET], in_groups(bank[5])))

            done = [0]

            def setup(ins):
                done[0] += 1
                ins.then_inc(s_dv0, 1)
                dve.wait_ge(s_dv0, done[0])

            v.memset(eps_col[:, :], EPS).then_inc(s_lw, 1)
            dve.wait_ge(s_w, 16 * 9)
            v.tensor_copy(loop_ext[:, 0:D], wload[:, 2, :]).then_inc(s_lw, 1)
            setup(v.tensor_copy(loop_ext[:, D:DX], att[:, 1:2]))
            setup(v.tensor_scalar(cap_b1[:, :], b1_col[:, :], -1.0, CAP, ALU.mult, ALU.add))
            dve.wait_ge(s_pe0, 2)
            setup(v.tensor_copy(w2_t[:, :], bank[1][:, 0:D]))
            for n, dest in enumerate((src_w, rel_w, fc1_t, w1_t)):
                v.tensor_copy(dest[:, 0:D], bank[0][:, n * D:(n + 1) * D]).then_inc(s_lw, 1)
            dve.wait_ge(s_pe0, 3)
            v.tensor_copy(dst_w[:, :], bank[2][:, 0:DX]).then_inc(s_lw, 1)
            v.tensor_copy(src_w[:, D:DX], bank[2][:, 256:257]).then_inc(s_lw, 1)
            v.tensor_copy(rel_w[:, D:DX], bank[2][:, 260:261]).then_inc(s_lw, 1)
            dve.wait_ge(s_pe0, 4)
            v.tensor_tensor(b2_fold[:, :], bank[3][:, 0:1], b2_col[:, :], ALU.add).then_inc(s_lw, 1)
            dve.wait_ge(s_lw, 10)
            v.tensor_scalar(cap_b2[:, :], b2_fold[:, :], -1.0, CAP, ALU.mult, ALU.add).then_inc(s_lw, 1)
            dve.wait_ge(s_lw, 11)
            v.memset(den[:, :, :, :], 1.0).then_inc(s_lw, 1)
            dve.wait_ge(s_lw, 12)
            v.memset(rden[:, :, :, :], 1.0).then_inc(s_wready, 1)

            def moments(grp, stat, steps, lt, tile):
                g, b, n, q, m = grp
                for t in range(lt):
                    tile(t)
                dve.wait_ge(stat, lt * (g + 1))
                mean_e, mean_o = stats[:, b, 0:lt, 1], stats[:, b, 0:lt, 4]
                dif, var = mdif[:, b, 0:lt], var4[:, b, 0:lt]
                v.tensor_tensor(dif, mean_e, mean_o, ALU.subtract).then_inc(steps, 1)
                v.tensor_tensor(var, stats[:, b, 0:lt, 2], stats[:, b, 0:lt, 5], ALU.add).then_inc(steps, 1)
                v.tensor_tensor(msum[:, b, 0:lt], mean_e, mean_o, ALU.add).then_inc(steps, 1)
                dve.wait_ge(steps, 5 * g + 1)
                v.tensor_tensor(dif, dif, dif, ALU.mult).then_inc(steps, 1)
                dve.wait_ge(steps, 5 * g + 4)
                v.scalar_tensor_tensor(out=var, in0=var, scalar=4.0 / D, in1=dif,
                                       op0=ALU.mult, op1=ALU.add).then_inc(steps, 1)

            def newton(grp, guessed, steps, lt, between=lambda k: None):
                g, b, n, q, m = grp
                y, u = guess[:, b, 0:lt], newt[:, b, 0:lt]
                dve.wait_ge(guessed, g + 1)
                v.tensor_tensor(u, y, y, ALU.mult).then_inc(steps, 1)
                between(0)
                dve.wait_ge(steps, 5 * g + 1)
                v.scalar_tensor_tensor(out=u, in0=var4[:, b, 0:lt], scalar=4 * EPS, in1=u,
                                       op0=ALU.add, op1=ALU.mult).then_inc(steps, 1)
                between(1)
                dve.wait_ge(steps, 5 * g + 2)
                v.tensor_scalar(u, u, -0.125, 1.5, ALU.mult, ALU.add).then_inc(steps, 1)
                between(2)
                dve.wait_ge(steps, 5 * g + 3)
                v.tensor_tensor(rstd[:, b, 0:lt], y, u, ALU.mult).then_inc(steps, 1)
                between(3)
                dve.wait_ge(steps, 5 * g + 4)
                v.scalar_tensor_tensor(out=nmr[:, b, 0:lt], in0=msum[:, b, 0:lt], scalar=-0.5,
                                       in1=rstd[:, b, 0:lt], op0=ALU.mult, op1=ALU.mult).then_inc(steps, 1)

            def take_moments(grp):
                g, b, n, q, m = grp
                dve.wait_ge(x_in[q], 16 * (m + 1))

                def tile(t):
                    if t == NT:
                        dve.wait_ge(got_src[b], 16 * ET * (n + 1))
                    if t == NT + ET:
                        dve.wait_ge(got_dst[b], 16 * ET * (n + 1))
                    v.bn_stats(stats[:, b, t, :], xn[:, q, t, :] if t < NT else xs[:, b, t - NT, :]).then_inc(s_stat, 1)

                moments(grp, s_stat, s_mom, LT, tile)

            def normalize(grp):
                g, b, n, q, m = grp
                newton(grp, s_guess, s_newt, LT)
                wait(dve, s_tp, 5 * (g - 1))
                dve.wait_ge(s_newt, 5 * (g + 1))
                for t in range(NT + SRC_ACT, LT):
                    v.tensor_scalar(normed[:, b, t, :], xs[:, b, t - NT, :],
                                    rstd[:, b, t:t + 1], nmr[:, b, t:t + 1], ALU.mult, ALU.add).then_inc(s_nd, 1)

            def combine_nodes(grp):
                g, b, n, q, m = grp
                dve.wait_ge(s_na, NORM_ACT * (g + 1))
                for half in range(2):
                    dve.wait_ge(s_nh, 2 * g + half + 1)
                    rows = xn[:, q, 4 * half:4 * half + 4, :].rearrange("p t d -> p (t d)")
                    v.scalar_tensor_tensor(out=rows, in0=NB[half][:, :], scalar=0.0, in1=rows,
                                           op0=ALU.max, op1=ALU.add).then_inc(s_x1, 1)

            def scores(grp):
                g, b, n, q, m = grp
                dve.wait_ge(s_mge, 4 * (g + 1))
                v.tensor_copy(score[:, :, bass.ds(g * ET, ET)],
                              mg[:, b, :, D].rearrange("p (k t) -> p k t", k=2)).then_inc(s_z, 1)
                dve.wait_ge(s_z, 2 * g + 1)
                v.memset(mg[:, b, 0:ET, D], 1.0).then_inc(s_z, 1)

            ran = [0]

            def run_step(ins):
                ran[0] += 1
                ins.then_inc(s_run, 1)
                dve.wait_ge(s_run, ran[0])

            def run_tables():
                dve.wait_ge(s_rows, 16 * 6)
                run_step(v.tensor_copy(row_b[:, :, :], nxt_i[:, :, :]))
                run_step(v.tensor_tensor(row_b[:, :, :], dst_f[:, :, :], row_b[:, :, :], ALU.is_equal))
                run_step(v.scalar_tensor_tensor(out=row_a[:, :, :], in0=row_b[:, :, ::-1], scalar=SKIP,
                                                in1=dst_f[:, :, ::-1], op0=ALU.mult, op1=ALU.add))
                run_step(v.tensor_copy(prev_f[:, :], prev_i[:, :]))
                run_step(v.tensor_copy(mirrored[:, :, :], dst_f[:, :, ::-1]))
                run_step(v.tensor_tensor(follows[:, :, :], dst_f[:, :, ::-1],
                                         prev_f[:, :].unsqueeze(2).broadcast_to([HALF, 2, P]), ALU.is_equal))
                run_step(v.memset(fresh[:, :, :], -FAR))
                run_step(v.tensor_tensor(fresh[:, :, 1:P], dst_f[:, :, 1:P], dst_f[:, :, 0:P - 1], ALU.not_equal))
                run_step(v.tensor_scalar(fresh[:, :, 1:P], fresh[:, :, 1:P], -FAR, None, ALU.mult))
                run_step(v.memset(fresh_back[:, :, :], -FAR))
                run_step(v.tensor_copy(fresh_back[:, :, 0:P - 1], fresh[:, :, 1:P]))

            def node_and_edge(at):
                if at(0) is None and at(-1) is not None:
                    run_tables()
                stage(normalize, at(1))
                stage(combine_nodes, at(-1))
                stage(scores, at(-1))
                stage(take_moments, at(2))

            staged(dve, GROUPS, -2, GROUPS, node_and_edge)

            dve.wait_ge(s_pe0, 5)
            run_step(v.tensor_copy(sidx[:, :], bank[6][:, 0:TILES]))
            dve.wait_ge(s_pe0, 6)
            run_step(v.tensor_copy(cols[:, :, 0], bank[7][:, 0:TILES]))

            count = [0]

            def sm(*instructions):
                for ins in instructions:
                    count[0] += 1
                    ins.then_inc(s_sm_dve, 1)
                dve.wait_ge(s_sm_dve, count[0])

            flat = "p h e -> p (h e)"
            dve.wait_ge(s_sm_pe, 1)
            zr = row_a
            sm(v.tensor_copy(zr[:, :, :].rearrange(flat), bank[0][0:HALF, 0:2 * P]))
            sm(v.tensor_tensor(row_b[:, :, :], zr[:, :, :], bank[0][0:HALF, 2 * P:4 * P]
                               .rearrange("p (h e) -> p h e", h=2)[:, :, ::-1], ALU.add))
            sm(v.scalar_tensor_tensor(out=zr[:, :, :], in0=row_b[:, :, :], scalar=0.01, in1=row_b[:, :, :],
                                      op0=ALU.mult, op1=ALU.max))

            def run_max(forward, backward):
                a, z = fresh[:, :, :].rearrange(flat), zr[:, :, :].rearrange(flat)
                ab = fresh_back[:, :, :].rearrange(flat)
                sm(v.tensor_tensor_scan(forward[:, :, :].rearrange(flat), a, z, -FAR, ALU.add, ALU.max))
                sm(v.tensor_tensor_scan(backward[:, :, :].rearrange(flat)[:, ::-1], ab[:, ::-1], z[:, ::-1], -FAR,
                                        ALU.add, ALU.max))

            run_max(fwd, bwd)
            assert count[0] + 1 == SM_BCAST
            for q, (column, source) in enumerate(((P - 1, dst_f), (0, dst_f), (P - 1, fwd), (0, bwd))):
                if q >= 2:
                    dve.wait_ge(s_sm_pe, q)
                sm(v.tensor_copy(spread[:, q % 2, :, :], source[:, :, column:column + 1].broadcast_to([HALF, 2, P])))
            dve.wait_ge(s_sm_pe, 5)
            sm(v.tensor_copy(tables[:, 0, :], bank[1][0:HALF, 0:2 * TILES]))
            sm(v.tensor_copy(tables[:, 1, :], bank[2][0:HALF, 0:2 * TILES]))
            sides = ((0, slice(0, TILES)), (P - 1, slice(TILES, 2 * TILES)))
            for h in range(2):
                sm(*[v.tensor_scalar(pick[:, k, :], tables[:, 0, of], dst_f[:, h, column:column + 1], -FAR,
                                     ALU.not_equal, ALU.mult) for k, (column, of) in enumerate(sides)])
                sm(*[v.tensor_tensor(pick[:, k, :], pick[:, k, :], tables[:, 1, of], ALU.add)
                     for k, (column, of) in enumerate(sides)])
                sm(*[v.tensor_reduce(best[:, k:k + 1], pick[:, k, :], AX.X, ALU.max) for k in range(2)])
                sm(*[v.tensor_tensor(zmax[:, h, k:k + 1], zr[:, h, column:column + 1], best[:, k:k + 1], ALU.max)
                     for k, (column, of) in enumerate(sides)])
            sm(v.tensor_copy(zkeep[:, :, :], zr[:, :, :]))
            sm(v.tensor_copy(zr[:, :, 0:1], zmax[:, :, 0:1]))
            sm(v.tensor_copy(zr[:, :, P - 1:P], zmax[:, :, 1:2]))
            run_max(fwd, bwd)
            sm(v.tensor_tensor(fwd[:, :, :], fwd[:, :, :], bwd[:, :, :], ALU.max))
            sm(v.tensor_tensor(row_a[:, :, :], zkeep[:, :, :], fwd[:, :, :], ALU.subtract))
            assert count[0] == SM_SHIFTED
            dve.wait_ge(s_sm_pe, 6)
            v.tensor_copy(cols[:, :, 1], bank[3][:, 0:TILES]).then_inc(s_cols, 1)
            dve.wait_ge(s_cols, 1)

            def copy_columns(grp, copied, used):
                g, b, n, q, m = grp
                wait(dve, used, ET * (g - 3))
                v.tensor_copy(colb[:, b, :, :], cols[:, bass.ds(g * ET, ET), :]).then_inc(copied, 1)

            def selection(grp, j, rows_in, copied, built, weighted):
                g, b, n, q, m = grp
                if j == 0:
                    dve.wait_ge(copied, g + 1)
                    dve.wait_ge(rows_in[b], 16 * (n + 1))
                row = drow[:, b, j * P:(j + 1) * P]
                if weighted:
                    v.tensor_scalar(same(q)[:, j, :], row, colb[:, b, j, 0:1], colb[:, b, j, 1:2],
                                    ALU.is_equal, ALU.mult).then_inc(built, 1)
                else:
                    v.tensor_scalar(same(q)[:, j, :], row, colb[:, b, j, 0:1], None,
                                    ALU.is_equal).then_inc(built, 1)

            def bound_weights(grp):
                g, b, n, q, m = grp
                dve.wait_ge(s_age, ET * (g + 1))
                for par in range(2):
                    v.tensor_scalar(den[:, b, par, :], sums_pair(b, par)[:, :, D], 1e-30, None, ALU.max).then_inc(s_den, 1)

            def invert_weights(grp):
                g, b, n, q, m = grp
                dve.wait_ge(s_den, 3 * g + 2)
                v.reciprocal(rden[:, b, :, :], den[:, b, :, :]).then_inc(s_den, 1)

            def take_shares(grp):
                g, b, n, q, m = grp
                dve.wait_ge(s_den, 3 * g + 3)
                for j in range(ET):
                    v.scalar_tensor_tensor(out=normed[:, b, j, :], in0=sums_at(b, j, D),
                                           scalar=rden[:, b, j % 2, j // 2:j // 2 + 1], in1=mg[:, q, ET + j, 0:D],
                                           op0=ALU.mult, op1=ALU.add).then_inc(s_at, 1)

            def finish_x1(grp):
                g, b, n, q, m = grp
                dve.wait_ge(s_at, ET * (g + 1))
                wait(dve, scattered[b], 16 * ET * n)
                wait(dve, kept1[b], 16 * n)
                v.scalar_tensor_tensor(out=x1b[:, b, 0:ET, :].rearrange("p t d -> p (t d)"),
                                       in0=normed[:, b, 0:ET, :].rearrange("p t d -> p (t d)"), scalar=0.0,
                                       in1=xdst[:, bass.ds(g * EG, EG)], op0=ALU.max, op1=ALU.add).then_inc(s_xo, 1)

            for b in range(2):
                dve.wait_ge(kept[b], 16 * SLOT_USES[b])
            for c in range(4):
                dve.wait_ge(x1_out[c], 16 * SLOT4_USES[c])
            dve.wait_ge(s_zero, 2)
            for b in range(2):
                dve.wait_ge(ea_out[b], 16 * SLOT_USES[b])

            def first_filter(grp):
                g, b, n, q, m = grp
                dve.wait_ge(s_p1, 3 * (g + 1))
                wait(dve, s_w2, g)
                v.scalar_tensor_tensor(out=soft[:, 2, :], in0=WB[0][b][:, :], scalar=b1_col[:, 0:1], in1=soft[:, 0, :],
                                       op0=ALU.add, op1=ALU.max).then_inc(s_sp1, 1)

            def second_filter(grp):
                g, b, n, q, m = grp
                dve.wait_ge(s_p2, 3 * (g + 1))
                wait(dve, filt_out[b], 16 * n)
                v.scalar_tensor_tensor(out=filt[:, b, :], in0=WB[1][b][:, :], scalar=b2_fold[:, 0:1], in1=soft[:, 1, :],
                                       op0=ALU.add, op1=ALU.max).then_inc(s_sp2, 1)

            def attend(at):
                stage(bound_weights, at(-1))
                stage(copy_columns, at(2), s_cb, s_ag)
                stage(invert_weights, at(-1))
                stage(selection, at(2), 0, dr_in, s_cb, s_sel, True)
                stage(take_shares, at(-1))
                for j in range(1, ET):
                    stage(selection, at(2), j, dr_in, s_cb, s_sel, True)
                stage(second_filter, at(-3))
                stage(finish_x1, at(-1))
                stage(first_filter, at(-1))

            staged(dve, GROUPS, -2, GROUPS + 2, attend, 3)

            for b in range(2):
                dve.wait_ge(kept1[b], 16 * SLOT_USES[b])

            def take_moments_x1(grp):
                g, b, n, q, m = grp
                dve.wait_ge(gathered1[q], 16 * ET * (m + 1))
                moments(grp, s_stat1, s_mom1, ET,
                        lambda t: v.bn_stats(stats[:, b, t, :], x1s(q, t)).then_inc(s_stat1, 1))

            def messages(grp):
                g, b, n, q, m = grp
                dve.wait_ge(s_f1, g + 1)
                dve.wait_ge(filt_in[b], 16 * (n + 1))
                wait(dve, s_tm, g)
                v.scalar_tensor_tensor(out=hT[:, 1, :], in0=filt[:, b, :], scalar=-LOG2, in1=bank[5][:, :],
                                       op0=ALU.add, op1=ALU.mult).then_inc(s_msg, 1)

            def add_sums(grp):
                g, b, n, q, m = grp
                dve.wait_ge(s_age1, ET * (g + 1))
                here = xdst[:, bass.ds(g * EG, EG)].rearrange("p (t d) -> p t d", d=D)
                for par in range(2):
                    tiles = here[:, par:ET:2, :]
                    v.tensor_tensor(tiles, tiles, sums_pair(b, par)[:, :, 0:D], ALU.add).then_inc(s_add1, 1)

            def convolve(at):
                def select(j):
                    stage(selection, at(-1), j, dr_in1, s_cb1, s_sel1, False)

                stage(copy_columns, at(-1), s_cb1, s_ag1)
                if at(1) is not None:
                    newton(at(1), s_guess1, s_newt1, ET, select)
                else:
                    for j in range(ET):
                        select(j)
                stage(add_sums, at(-4))
                stage(take_moments_x1, at(2))
                stage(messages, at(0))

            staged(dve, GROUPS, -2, GROUPS + 3, convolve, 4)


_INS = ["x", "src", "dst", "edge_attr_128", "L0_gnn_w", "L0_gnn_w_r", "L0_gnn_att_w", "L0_gnn_loop_w",
        "L1_gnn_fc1_w", "L1_gnn_w1", "L1_gnn_b1", "L1_gnn_w2", "L1_gnn_b2"]


def kernel(**inputs):
    import concourse.bacc as bacc
    import numpy as np
    from concourse.bass_utils import run_bass_kernel_spmd

    nc = bacc.Bacc("TRN2", target_bir_lowering=False, num_devices=1)
    arrays, args = {}, []
    for name in _INS:
        a = np.ascontiguousarray(inputs[name])
        arrays[f"in_{name}"] = a
        args.append(nc.dram_tensor(f"in_{name}", a.shape, mybir.dt.from_np(a.dtype), kind="ExternalInput").ap())
    out = nc.dram_tensor("out_x", inputs["x"].shape, F32, kind="ExternalOutput").ap()
    gnn_kernel(nc, *args, out)
    result = run_bass_kernel_spmd(nc, [arrays], core_ids=[0])
    return result.results[0]["out_x"]
```
